# Optimizing a Trainium2 kernel written in Bass

```python
import numpy as np
import jax
import jax.numpy as jnp

def _softmax(x, axis=-1):
    return jax.nn.softmax(x, axis=axis)

def _gelu(x):
    return jax.nn.gelu(x, approximate=True)

def _silu(x):
    return jax.nn.silu(x)

def _sigmoid(x):
    return jax.nn.sigmoid(x)

def _layernorm(x, axis=-1, eps=1e-05):
    m = jnp.mean(x, axis=axis, keepdims=True)
    v = jnp.var(x, axis=axis, keepdims=True)
    return (x - m) / jnp.sqrt(v + eps)

def _scatter_add(tgt, idx, src, axis=0):
    return tgt.at[idx].add(src)

def _segment_sum(src, seg, n):
    return jax.ops.segment_sum(src, seg, n)
kernel_name = 'mk_decoder_preln_d1_seqx_r4_0c82c5'

def setup_inputs(seed: int=0):
    np.random.seed(seed)
    _w = jnp.asarray

    def _rec_inputs():
        import jax
        import jax.numpy as jnp
        _rk = jax.random.key(seed)
        x = -0.0002928 + 1 * jax.random.normal(jax.random.fold_in(_rk, 1), (16, 128, 256), jnp.float32)
        _lenS = 128 - jax.random.randint(jax.random.fold_in(_rk, 7), (16,), 0, max(1, 128 // 4) + 1, jnp.int32)
        _lenS2 = 128 - jax.random.randint(jax.random.fold_in(_rk, 8), (16,), 0, max(1, 128 // 4) + 1, jnp.int32)
        _ctx_1024P = jax.random.normal(jax.random.fold_in(_rk, 11), (16, 16, 256), jnp.float32)
        _ctx_1024c = jax.random.dirichlet(jax.random.fold_in(_rk, 511), 0.3 * jnp.ones((16,), jnp.float32), (16, 128))
        _ctx_1024t = jnp.einsum('bsk,bkd->bsd', _ctx_1024c, _ctx_1024P)
        _ctx_1024t = _ctx_1024t * jax.lax.rsqrt(jnp.mean(jnp.square(_ctx_1024t)) + 1e-12) * 0.953939
        ctx_1024 = -1.39393e-06 + 0.999914 * (_ctx_1024t + 0.3 * jax.random.normal(jax.random.fold_in(_rk, 611), (16, 128, 256), jnp.float32))
        _validS = jnp.arange(128)[None, :] < _lenS[:, None]
        _validS2 = jnp.arange(128)[None, :] < _lenS2[:, None]
        _causal = jnp.tril(jnp.ones((128, 128), dtype=bool))
        mask_1x1xSxS2_bk0 = jnp.logical_not(jnp.broadcast_to(_validS2[0:1, None, None, :], (1, 1, 128, 128)))
        return (x, ctx_1024, mask_1x1xSxS2_bk0)
    x, ctx_1024, mask_1x1xSxS2_bk0 = _rec_inputs()

    def _L0_attn_setup():
        import jax, jax.numpy as jnp
        import numpy as np
        B, T, D = (4, 512, 256)
        H, Dh = (16, 64)
        key = jax.random.key(seed)
        ks = jax.random.split(key, 5)
        std_qkv = float(np.sqrt(2.0 / (Dh * D)))
        std_o = float(np.sqrt(2.0 / (D * Dh)))
        return {'x': jax.random.normal(ks[0], (B, T, D), dtype=jnp.float32), 'W_Q': jax.random.normal(ks[1], (H, Dh, D), dtype=jnp.float32) * std_qkv, 'b_Q': jnp.zeros((H, Dh), dtype=jnp.float32), 'W_K': jax.random.normal(ks[2], (H, Dh, D), dtype=jnp.float32) * std_qkv, 'b_K': jnp.zeros((H, Dh), dtype=jnp.float32), 'W_V': jax.random.normal(ks[3], (H, Dh, D), dtype=jnp.float32) * std_qkv, 'b_V': jnp.zeros((H, Dh), dtype=jnp.float32), 'W_O': jax.random.normal(ks[4], (H, D, Dh), dtype=jnp.float32) * std_o, 'b_O': jnp.zeros((D,), dtype=jnp.float32)}
    _L0_attn_all = _L0_attn_setup()
    _L0_attn_in = {k: v for k, v in _L0_attn_all.items() if k in ('W_Q', 'b_Q', 'W_K', 'b_K', 'W_V', 'b_V', 'W_O', 'b_O')}
    del _L0_attn_all

    def _L0_xattn_setup():
        import jax, jax.numpy as jnp
        import numpy as np
        import math
        D_MODEL = 256
        NUM_HEADS = 16
        D_K = D_MODEL // NUM_HEADS
        key = jax.random.key(seed)
        ks = jax.random.split(key, 12)
        B, S = (2, 512)
        s = 1.0 / math.sqrt(D_MODEL)
        inp = {'q': jax.random.normal(ks[0], (B, S, D_MODEL), jnp.float32), 'k': jax.random.normal(ks[1], (B, S, D_MODEL), jnp.float32), 'v': jax.random.normal(ks[2], (B, S, D_MODEL), jnp.float32), 'mask': jnp.tril(jnp.ones((S, S), dtype=bool))[None, None, :, :], 'Wq': jax.random.normal(ks[3], (D_MODEL, D_MODEL), jnp.float32) * s, 'bq': jax.random.normal(ks[4], (D_MODEL,), jnp.float32) * s, 'Wk': jax.random.normal(ks[5], (D_MODEL, D_MODEL), jnp.float32) * s, 'bk': jax.random.normal(ks[6], (D_MODEL,), jnp.float32) * s, 'Wv': jax.random.normal(ks[7], (D_MODEL, D_MODEL), jnp.float32) * s, 'bv': jax.random.normal(ks[8], (D_MODEL,), jnp.float32) * s, 'Wo': jax.random.normal(ks[9], (D_MODEL, D_MODEL), jnp.float32) * s, 'bo': jax.random.normal(ks[10], (D_MODEL,), jnp.float32) * s}
        return inp
    _L0_xattn_all = _L0_xattn_setup()
    _L0_xattn_in = {k: v for k, v in _L0_xattn_all.items() if k in ('Wq', 'bq', 'Wk', 'bk', 'Wv', 'bv', 'Wo', 'bo')}
    del _L0_xattn_all

    def _L0_ffn_setup():
        import jax, jax.numpy as jnp
        import numpy as np
        TEMPERATURE = 0.5
        CAPACITY_FACTOR = 1.25
        TOP_K = 1
        key = jax.random.key(seed)
        ks = jax.random.split(key, 5)
        B, S, D, H, E = (4, 512, 256, 512, 8)
        s = 0.02
        return {'x': jax.random.normal(ks[0], (B, S, D), jnp.float32), 'gate_w': jax.random.normal(ks[1], (E, D), jnp.float32) * s, 'gate_b': jnp.zeros((E,), jnp.float32), 'rms_w': jnp.ones((E,), jnp.float32), 'w1': jax.random.normal(ks[2], (E, D, H), jnp.float32) * s, 'b1': jnp.zeros((E, H), jnp.float32), 'w2': jax.random.normal(ks[3], (E, H, D), jnp.float32) * s, 'b2': jnp.zeros((E, D), jnp.float32)}
    _L0_ffn_all = _L0_ffn_setup()
    _L0_ffn_in = {k: v for k, v in _L0_ffn_all.items() if k in ('gate_w', 'gate_b', 'rms_w', 'w1', 'b1', 'w2', 'b2')}
    del _L0_ffn_all
    return {'x': x, 'ctx_1024': ctx_1024, 'mask_1x1xSxS2_bk0': mask_1x1xSxS2_bk0, 'L0_attn_W_Q': _L0_attn_in['W_Q'], 'L0_attn_b_Q': _L0_attn_in['b_Q'], 'L0_attn_W_K': _L0_attn_in['W_K'], 'L0_attn_b_K': _L0_attn_in['b_K'], 'L0_attn_W_V': _L0_attn_in['W_V'], 'L0_attn_b_V': _L0_attn_in['b_V'], 'L0_attn_W_O': _L0_attn_in['W_O'], 'L0_attn_b_O': _L0_attn_in['b_O'], 'L0_xattn_Wq': _L0_xattn_in['Wq'], 'L0_xattn_bq': _L0_xattn_in['bq'], 'L0_xattn_Wk': _L0_xattn_in['Wk'], 'L0_xattn_bk': _L0_xattn_in['bk'], 'L0_xattn_Wv': _L0_xattn_in['Wv'], 'L0_xattn_bv': _L0_xattn_in['bv'], 'L0_xattn_Wo': _L0_xattn_in['Wo'], 'L0_xattn_bo': _L0_xattn_in['bo'], 'L0_ffn_gate_w': _L0_ffn_in['gate_w'], 'L0_ffn_gate_b': _L0_ffn_in['gate_b'], 'L0_ffn_rms_w': _L0_ffn_in['rms_w'], 'L0_ffn_w1': _L0_ffn_in['w1'], 'L0_ffn_b1': _L0_ffn_in['b1'], 'L0_ffn_w2': _L0_ffn_in['w2'], 'L0_ffn_b2': _L0_ffn_in['b2']}

def reference(x, ctx_1024, mask_1x1xSxS2_bk0, L0_attn_W_Q, L0_attn_b_Q, L0_attn_W_K, L0_attn_b_K, L0_attn_W_V, L0_attn_b_V, L0_attn_W_O, L0_attn_b_O, L0_xattn_Wq, L0_xattn_bq, L0_xattn_Wk, L0_xattn_bk, L0_xattn_Wv, L0_xattn_bv, L0_xattn_Wo, L0_xattn_bo, L0_ffn_gate_w, L0_ffn_gate_b, L0_ffn_rms_w, L0_ffn_w1, L0_ffn_b1, L0_ffn_w2, L0_ffn_b2):
    import jax
    import jax.numpy as jnp

    def _L0_attn_ref(x, W_Q, b_Q, W_K, b_K, W_V, b_V, W_O, b_O):
        import jax, jax.numpy as jnp
        import numpy as np
        B, T, D = (4, 512, 256)
        H, Dh = (16, 64)
        Q = jnp.einsum('btd,hkd->bthk', x, W_Q) + b_Q
        K = jnp.einsum('btd,hkd->bthk', x, W_K) + b_K
        V = jnp.einsum('btd,hkd->bthk', x, W_V) + b_V
        d_head = W_Q.shape[1]
        scores = jnp.einsum('bqhk,bshk->bhqs', Q, K) / jnp.sqrt(jnp.asarray(d_head, x.dtype))
        attn = jax.nn.softmax(scores, axis=-1)
        out_h = jnp.einsum('bhqs,bshk->bqhk', attn, V)
        return jnp.einsum('bqhk,hdk->bqd', out_h, W_O) + b_O

    def _L0_xattn_ref(q, k, v, mask, Wq, bq, Wk, bk, Wv, bv, Wo, bo):
        import jax, jax.numpy as jnp
        import numpy as np
        import math
        D_MODEL = 256
        NUM_HEADS = 16
        D_K = D_MODEL // NUM_HEADS
        B, S, _ = q.shape

        def proj(x, W, b):
            y = x @ W.T + b
            return y.reshape(B, -1, NUM_HEADS, D_K).transpose(0, 2, 1, 3)
        Q = proj(q, Wq, bq)
        K = proj(k, Wk, bk)
        V = proj(v, Wv, bv)
        scores = jnp.einsum('bhqd,bhkd->bhqk', Q, K) / math.sqrt(D_K)
        scores = jnp.where(mask, scores, jnp.float32(-1000000000.0))
        probs = jax.nn.softmax(scores, axis=-1)
        attn = jnp.einsum('bhqk,bhkd->bhqd', probs, V)
        attn = attn.transpose(0, 2, 1, 3).reshape(B, S, D_MODEL)
        return attn @ Wo.T + bo

    def _L0_ffn_ref(x, gate_w, gate_b, rms_w, w1, b1, w2, b2):
        import jax, jax.numpy as jnp
        import numpy as np
        TEMPERATURE = 0.5
        CAPACITY_FACTOR = 1.25
        TOP_K = 1
        B, S, D = x.shape
        E = gate_w.shape[0]
        xf = x.reshape(-1, D)
        N = xf.shape[0]
        logits = xf @ gate_w.T + gate_b
        eps = jnp.finfo(logits.dtype).eps
        ms = jnp.mean(logits * logits, axis=-1, keepdims=True)
        logits = logits * jax.lax.rsqrt(ms + eps) * rms_w
        gates = jax.nn.softmax(logits / TEMPERATURE, axis=-1)
        g, idx = jax.lax.top_k(gates, TOP_K)
        g, idx = (g[:, 0], idx[:, 0])
        capacity = min(int(np.ceil(N * TOP_K / E * CAPACITY_FACTOR)), N)
        counts = jnp.zeros((E,), jnp.int32).at[idx].add(1)
        active = (counts > 0) & (capacity >= 1)
        mask = active[idx].astype(gates.dtype)
        masked = g * mask
        norm_g = masked / (masked + 1e-06)
        h = jax.nn.gelu(jnp.einsum('nd,edh->neh', xf, w1) + b1, approximate=False)
        y = jnp.einsum('neh,ehd->ned', h, w2) + b2
        out = (y * norm_g[:, None, None]).sum(axis=1)
        return out.reshape(B, S, D)
    x = x + _L0_attn_ref(_layernorm(x, axis=-1), L0_attn_W_Q, L0_attn_b_Q, L0_attn_W_K, L0_attn_b_K, L0_attn_W_V, L0_attn_b_V, L0_attn_W_O, L0_attn_b_O)
    x = x + _L0_xattn_ref(_layernorm(x, axis=-1), ctx_1024, ctx_1024, mask_1x1xSxS2_bk0, L0_xattn_Wq, L0_xattn_bq, L0_xattn_Wk, L0_xattn_bk, L0_xattn_Wv, L0_xattn_bv, L0_xattn_Wo, L0_xattn_bo)
    x = x + _L0_ffn_ref(_layernorm(x, axis=-1), L0_ffn_gate_w, L0_ffn_gate_b, L0_ffn_rms_w, L0_ffn_w1, L0_ffn_b1, L0_ffn_w2, L0_ffn_b2)
    return x

_drawn_inputs = setup_inputs


def setup_inputs(seed=0):
    import zlib

    import numpy as np

    out = dict(_drawn_inputs(seed))
    spreads = {'L0_attn_b_Q': (0.0, 0.8),
     'L0_attn_b_K': (0.0, 0.8),
     'L0_attn_b_V': (0.0, 0.27),
     'L0_attn_b_O': (0.0, 0.1),
     'L0_ffn_gate_b': (0.0, 0.8),
     'L0_ffn_rms_w': (1.0, 0.6),
     'L0_ffn_b1': (0.0, 0.1),
     'L0_ffn_b2': (0.0, 0.1)}
    factors = {'L0_attn_W_Q': 8.0, 'L0_attn_W_K': 8.0, 'L0_attn_W_V': 8.0, 'L0_ffn_gate_w': 8.0}
    for name, (base, spread) in spreads.items():
        noise = np.random.default_rng([zlib.crc32(name.encode()), seed]).standard_normal(out[name].shape)
        drawn = base * np.exp(spread * noise) if base else spread * noise
        out[name] = jnp.asarray(drawn.astype(out[name].dtype))
    for name, factor in factors.items():
        out[name] = (out[name] * factor).astype(out[name].dtype)
    return out
```

```python
from collections import namedtuple
from contextlib import ExitStack

import concourse.bass as bass
from concourse import mybir

F32 = mybir.dt.float32
F32R = mybir.dt.float32r
U8 = mybir.dt.uint8
ALU = mybir.AluOpType
ACT = mybir.ActivationFunctionType
AX = mybir.AxisListType

P = 128
D = 256
KD = D // P
GROUPS = 4
TILES = 4
GT = TILES * P
QUADS = 16
SLOTS = QUADS + 4
HEADS = 16
DH1, DH2 = 64, 16
CHUNKS1 = HEADS * DH1 // P
EXPERTS, HID = 8, 512
MCH = EXPERTS * HID // P
PIECE = 512
N1, N2 = 16, 4
HALF = MCH // 2
LN_EPS = 1e-5
F32_EPS = 1.1920928955078125e-07
MASKED = -1e9

BQ1, BK1, BV1 = 0, 8, 16
BQ2, BK2, BV2, B1 = 32, 34, 36, 38
NBIAS = B1 + MCH

Count = namedtuple("Count", "credit per")


def nth(count, ph, g, i):
    return count.credit + GROUPS * sum(count.per[:ph]) + g * count.per[ph] + i + 1


SLOT = Count(0, (16, 16, 0))
SLOT_F1 = Count(1, (16, 16, 0))
SLOT_F2 = Count(2, (16, 16, 0))
SLOT_F4 = Count(4, (16, 16, 0))
QK = Count(0, (16, 4, 0))
QK_F1 = Count(1, (16, 4, 0))
VJ = Count(0, (16, 4, 0))
VJ_F2 = Count(2, (16, 4, 0))
ATC = Count(0, (0, 2, 0))
ATC_F2 = Count(2, (0, 2, 0))
OPROJ = Count(2, (8, 2, 0))
GRP = Count(0, (1, 1, 1))
GRP_F1 = Count(1, (1, 1, 1))
CTX = Count(0, (0, 1, 0))
MSTEP = Count(0, (0, 0, MCH))
MSTEP_F2 = Count(2, (0, 0, MCH))
MSTEP_F4 = Count(4, (0, 0, MCH))
LNST = Count(0, (TILES, TILES, TILES))


def build(nc, x, ctxT, mask, pieces, gateT, biases, rows, out):
    with ExitStack() as ctx:
        def sb(name, shape, dt):
            return ctx.enter_context(nc.sbuf_tensor(name, shape, dt))

        def bank(name):
            return ctx.enter_context(nc.psum_tensor(name, [P, 512], F32))

        def sem(name):
            return ctx.enter_context(nc.semaphore(name))

        arena = sb("arena", [P, MCH * 2 * PIECE], F32R)
        work = (N1 + N2) * 2 * PIECE

        def piece(i, lo, k, a, b):
            at = i * 2 * PIECE + lo * PIECE + k * 256
            return arena[:, at + a:at + b]

        def region(cols):
            nonlocal work
            at = work
            work += cols
            return arena[:, at:at + cols]

        V = region(4096).rearrange("p (r s t c) -> p r s t c", r=2, s=2, t=TILES)
        K = region(4096).rearrange("p (r s b h c) -> p r s b h c", r=2, s=2, b=TILES, h=2)
        Q = region(2048).rearrange("p (r s c) -> p r s c", r=2, s=2)
        AT = region(2048).rearrange("p (r s c) -> p r s c", r=2, s=2)
        assert work == MCH * 2 * PIECE

        PT = sb("PT", [P, 2, 2, 512], F32R)
        XT = sb("XT", [P, 2, KD, GT], F32R)
        CT = sb("CT", [P, 2, KD, GT], F32R)
        gate = sb("gate", [P, 2, KD * EXPERTS], F32R)
        probs = sb("probs", [P, 4, 512], F32)
        xs = sb("xs", [P, GROUPS * TILES, D], F32)
        xn = sb("xn", [P, TILES, D], F32)
        craw = sb("craw", [P, KD * GT], F32)
        yo = craw[:, :].rearrange("p (t d) -> p t d", t=TILES)
        wst = sb("wst", [P, 4, PIECE], F32)
        araw = sb("araw", [P, 2, GT], F32)
        ident = sb("ident", [P, P], F32)
        bias = sb("bias", [P, NBIAS], F32)
        rowc = sb("rowc", [P, 2 * D + 2 * EXPERTS], F32)
        b2sum = sb("b2sum", [P, D], F32)
        gst = sb("gst", [P, KD * EXPERTS], F32)
        msk = sb("msk", [P, P], U8)
        dropped = sb("dropped", [P, P], U8)
        neg = sb("neg", [P, 1], F32)
        half = sb("half", [P, 2], F32)
        bkh = sb("bkh", [P, 4], F32)
        mhalf = sb("mhalf", [P, TILES], F32)
        nm = sb("nm", [P, 4, 4], F32)
        rsum = sb("rsum", [P, 4, 4], F32)
        rinv = sb("rinv", [P, 4, 4], F32)
        st = sb("st", [P, TILES, 6], F32)
        mv = sb("mv", [P, TILES, 2], F32)
        ve = sb("ve", [P, TILES], F32)
        rstd = sb("rstd", [P, TILES], F32)
        lg = sb("lg", [P, 5, TILES * EXPERTS], F32)
        gs = sb("gs", [P, 8, TILES], F32)
        b2raw = probs[:, :, :].rearrange("p r c -> p (r c)")

        A0, A1, S0, S1, T, O, Y0, Y1 = (bank(n) for n in ("A0", "A1", "S0", "S1", "T", "O", "Y0", "Y1"))
        A, S, Y = (A0, A1), (S0, S1), (Y0, Y1)
        H = (S0, S1, A0, A1)

        x_in = sem("x_in")
        b_in = sem("b_in")
        c_in = sem("c_in")
        w_in = [sem(f"w_in{i}") for i in range(4)]
        out_dma = sem("out_dma")
        ready = sem("ready")
        ready_v = sem("ready_v")
        w_hi = sem("w_hi")
        w_split = sem("w_split")
        e_hi = sem("e_hi")
        e_split = sem("e_split")
        scores_ps = sem("scores_ps")
        filled = sem("filled")
        maxed = sem("maxed")
        exped = sem("exped")
        inverted = sem("inverted")
        normed = sem("normed")
        pt_ps = sem("pt_ps")
        pt_hi = sem("pt_hi")
        pt_lo = sem("pt_lo")
        pv_ps = sem("pv_ps")
        o_hi = sem("o_hi")
        o_lo = sem("o_lo")
        at_hi = sem("at_hi")
        at_lo = sem("at_lo")
        oproj = sem("oproj")
        qk_ps = sem("qk_ps")
        qk_hi = sem("qk_hi")
        qk_lo = sem("qk_lo")
        v_ps = sem("v_ps")
        v_hi = sem("v_hi")
        v_lo = sem("v_lo")
        xt_ps = sem("xt_ps")
        xt_hi = sem("xt_hi")
        xt_lo = sem("xt_lo")
        c_hi = sem("c_hi")
        c_lo = sem("c_lo")
        y_read = sem("y_read")
        x_ready = sem("x_ready")
        ln_stat = sem("ln_stat")
        ln_aggr = sem("ln_aggr")
        ln_var = sem("ln_var")
        ln_rstd = sem("ln_rstd")
        ln_x = sem("ln_x")
        f1_ps = sem("f1_ps")
        act_done = sem("act_done")
        h_hi = sem("h_hi")
        h_lo = sem("h_lo")
        f2_ps = sem("f2_ps")
        lg_ps = sem("lg_ps")
        lg_v = sem("lg_v")
        lg_pow = sem("lg_pow")
        lg_exp = sem("lg_exp")
        y_sum = sem("y_sum")
        fin = sem("fin")
        kbias = sem("kbias")
        ng_done = sem("ng_done")
        pe_gate = sem("pe_gate")
        dve_gate = sem("dve_gate")
        pool_gate = sem("pool_gate")
        LGV = 12

        def v_jobs(ph, n):
            if ph == 0 and 1 <= n <= 12:
                return [((n - 1) % 4, (n - 1) // 4 + 1)]
            return []

        def qk_jobs(ph, n):
            if ph == 0 and n <= 13:
                return [n + 2]
            if ph == 1 and n in (4, 5):
                return [n - 2]
            return []

        XT_SLOT = (14, 8)
        CT_SLOT = 8

        def next_q(ph, n):
            return {(0, 15): 0, (0, 16): 1, (1, 12): 0, (1, 13): 1}.get((ph, n))

        def next_v(ph, n):
            return {16: (0,), 17: (1,), 18: (2,), 19: (3,)}.get(n, ()) if ph == 0 else \
                {17: (0, 1), 18: (2, 3)}.get(n, ())

        def following(ph, g):
            if isinstance(g, int) and g == GROUPS - 1:
                return (ph + 1, 0)
            return (ph, g + 1)

        block = ctx.enter_context(nc.Block())

        @block.sync
        def _(sp):
            for g in range(GROUPS):
                sp.dma_start(xs[:, TILES * g:TILES * (g + 1), :], x[g]).then_inc(x_in, 16)
                if g == 0:
                    for i in range(4):
                        sp.dma_start(wst[:, i, :], pieces[i]).then_inc(w_in[i], 16)
            for i in range(4, N1 + N2):
                sp.wait_ge(w_split, i - 3)
                sp.dma_start(wst[:, i % 4, :], pieces[i]).then_inc(w_in[i % 4], 16)

            def context(g):
                sp.dma_start(craw[:, :].rearrange("p (k t) -> p k t", k=KD),
                             ctxT[g]).then_inc(c_in, 16)

            def experts(g):
                for j in range(4):
                    if isinstance(g, int) and g == 0:
                        sp.wait_ge(w_split, N1 + N2 - 3 + j)
                    else:
                        sp.wait_ge(e_split, g * 4 + j - 3)
                    sp.dma_start(wst[:, j, :], pieces[N1 + N2 + g * 4 + j]).then_inc(w_in[j], 16)

            context(0)
            experts(0)
            with sp.Fori(1, GROUPS) as g:
                sp.wait_ge(c_lo, nth(CTX, 1, g, -1))
                context(g)
                experts(g)
            with sp.Fori(GROUPS, 2 * GROUPS) as g:
                experts(g)
            with sp.Fori(0, GROUPS) as g:
                sp.wait_ge(fin, g + 1)
                sp.dma_start(out[g], yo).then_inc(out_dma, 16)
            sp.wait_ge(out_dma, GROUPS * 16)

        @block.tensor
        def _(pe):
            def three(acc, lhs, rhs, first=True, last=True, shared=False):
                for i, (a, b) in enumerate(((0, 0), (0, 1), (1, 0))):
                    mm = pe.matmul(acc, lhs[a], rhs[b], start=first and i == 0,
                                   stop=last and i == 2, skip_group_check=shared)
                return mm

            def project_qk(ph, g, job):
                c, is_k = job // 2, job % 2
                pe.wait_ge(qk_lo, nth(QK_F1, ph, g, job - 1))
                if ph == 1 and job == 2:
                    pe.wait_ge(v_lo, nth(VJ_F2, ph, g, 3))
                if job == 0:
                    pe.wait_ge(xt_lo, nth(GRP, ph, g, 0))
                if ph == 1 and job == 1:
                    pe.wait_ge(c_lo, nth(CTX, 1, g, 0))
                i = 4 * (c // 2) + is_k if ph == 0 else N1 + is_k
                col = (c % 2) * P
                pe.wait_ge(w_split, i + 1)
                src = CT if ph == 1 and is_k else XT
                for k in range(KD):
                    mm = three(A0[:, :], [piece(i, s, k, col, col + P) for s in (0, 1)],
                               [src[:, s, k, :] for s in (0, 1)], k == 0, k == KD - 1)
                mm.then_inc(qk_ps, 1)

            def project_v(ph, g, cp, t):
                job = 4 * cp + t
                to = A1 if ph == 0 or t % 2 == 0 else A0
                if ph == 0:
                    pe.wait_ge(v_lo, nth(VJ_F2, ph, g, job - 1))
                    if job == 0:
                        pe.wait_ge(xt_lo, nth(GRP, ph, g, 0))
                else:
                    pe.wait_ge(v_lo, nth(VJ_F2, ph, g, job - 2 if t > 1 else -1))
                    if t == 1:
                        pe.wait_ge(qk_lo, nth(QK_F1, ph, g, 1))
                i = 4 * cp + 2 if ph == 0 else N1 + 2
                pe.wait_ge(w_split, i + 1)
                src = XT if ph == 0 else CT
                for k in range(KD):
                    mm = three(to[:, 0:256], [src[:, s, k, t * P:(t + 1) * P] for s in (0, 1)],
                               [piece(i, s, k, 0, 256) for s in (0, 1)], k == 0, k == KD - 1)
                mm.then_inc(v_ps, 1)

            def scores(ph, g, n):
                c = n // 2
                if ph == 0:
                    r, rows = c % 2, slice(0, P)
                    if n % 2 == 0:
                        pe.wait_ge(qk_lo, nth(QK_F1, ph, g, 2 * c + 1))
                else:
                    r, rows = c // 4, slice(32 * (c % 4), 32 * (c % 4) + 32)
                    if n % 8 == 0:
                        pe.wait_ge(qk_lo, nth(QK_F1, ph, g, 2 * r + 1))
                pe.wait_ge(exped, nth(SLOT_F2, ph, g, n - 2))
                if ph == 1:
                    pe.sem_inc(pe_gate, 1)
                for j in range(2):
                    b = 2 * (n % 2) + j
                    mm = three(S[n % 2][:, 256 * j:256 * (j + 1)],
                               [Q[rows, r, s, b * P:(b + 1) * P] for s in (0, 1)],
                               [K[rows, r, s, b, :, :].rearrange("p h c -> p (h c)") for s in (0, 1)])
                mm.then_inc(scores_ps, 1)

            def transpose_probs(ph, g, n):
                pe.wait_ge(normed, nth(SLOT, ph, g, n))
                pe.wait_ge(pt_lo, nth(SLOT_F1, ph, g, n - 1))
                for u in range(4):
                    mm = pe.transpose(T[:, u * P:(u + 1) * P], probs[:, n % 4, u * P:(u + 1) * P],
                                      ident[:, :])
                mm.then_inc(pt_ps, 1)

            def probs_v(ph, g, n):
                c = n // 2
                pe.wait_ge(pt_lo, nth(SLOT_F1, ph, g, n))
                pe.wait_ge(o_lo, nth(SLOT_F1, ph, g, n - 1))
                if ph == 0:
                    cp = c // 2
                    if n % 4 < 2:
                        pe.wait_ge(v_lo, nth(VJ_F2, ph, g, 4 * cp + 2 * (n % 2) + 1))
                    for u in range(4):
                        b, h = 2 * (n % 2) + u // 2, u % 2
                        col = (c % 2) * P + h * DH1
                        mm = three(O[0:DH1, u * P:(u + 1) * P],
                                   [V[:, cp % 2, s, b, col:col + DH1] for s in (0, 1)],
                                   [PT[:, n % 2, s, u * P:(u + 1) * P] for s in (0, 1)])
                else:
                    if n < 2:
                        pe.wait_ge(v_lo, nth(VJ_F2, ph, g, 2 * (n % 2) + 1))
                    for j in range(2):
                        b = 2 * (n % 2) + j
                        mm = three(O[0:32, j * 256:(j + 1) * 256],
                                   [V[:, 0, s, b, 32 * c:32 * c + 32] for s in (0, 1)],
                                   [PT[:, n % 2, s, j * 256:(j + 1) * 256] for s in (0, 1)])
                mm.then_inc(pv_ps, 1)

            def project_out(ph, g, c, tiles):
                chunks = CHUNKS1 if ph == 0 else 2
                if ph == 0:
                    pe.wait_ge(o_lo, nth(SLOT_F1, ph, g, 2 * c + tiles[0] // 2))
                    i, k = 4 * (c // 2) + 3, c % 2
                else:
                    pe.wait_ge(at_lo, nth(ATC_F2, ph, g, c))
                    i, k = N1 + 3, c
                if c == 0:
                    pe.wait_ge(y_read, nth(GRP_F1, ph, g, -1))
                pe.wait_ge(w_split, i + 1)
                for t in tiles:
                    mm = three(Y[t // 2][:, (t % 2) * D:(t % 2 + 1) * D],
                               [AT[:, c % 2, s, t * P:(t + 1) * P] for s in (0, 1)],
                               [piece(i, s, k, 0, D) for s in (0, 1)],
                               c == 0 and t % 2 == 0, c == chunks - 1, True)
                if tiles[-1] == TILES - 1:
                    mm.then_inc(oproj, 1)

            def transpose_tokens(ph, g, banks):
                pe.wait_ge(ln_x, nth(GRP, ph, g, 0))
                for k in range(KD):
                    for t in range(TILES):
                        mm = pe.transpose(banks[k][:, t * P:(t + 1) * P], xn[:, t, k * P:(k + 1) * P],
                                          ident[:, :])
                mm.then_inc(xt_ps, 1)

            pe.wait_ge(ready, 2)
            transpose_tokens(0, 0, A)
            project_qk(0, 0, 0)
            project_qk(0, 0, 1)
            for t in range(TILES):
                project_v(0, 0, 0, t)

            def attention(ph, g):
                nph, ng = following(ph, g)
                for n in range(SLOTS):
                    if n < QUADS:
                        scores(ph, g, n)
                    for job in qk_jobs(ph, n):
                        project_qk(ph, g, job)
                    if nph < 2 and next_q(ph, n) is not None:
                        project_qk(nph, ng, next_q(ph, n))
                    if 1 <= n <= QUADS:
                        transpose_probs(ph, g, n - 1)
                    if 2 <= n <= QUADS + 1:
                        probs_v(ph, g, n - 2)
                    for t, cp in v_jobs(ph, n):
                        project_v(ph, g, cp, t)
                    if nph < 2:
                        for t in next_v(ph, n):
                            project_v(nph, ng, 0, t)
                    if ph == 0 and n >= 4:
                        project_out(ph, g, (n - 4) // 2, (0, 1) if n % 2 == 0 else (2, 3))
                    if ph == 1 and n in (11, 12, 18, 19):
                        project_out(ph, g, 0 if n < 16 else 1, (0, 1) if n in (11, 18) else (2, 3))
                    if n == XT_SLOT[ph]:
                        pe.wait_ge(qk_lo, nth(QK_F1, ph, g, QK.per[ph] - 1))
                        pe.wait_ge(v_lo, nth(VJ_F2, ph, g, VJ.per[ph] - 1))
                        transpose_tokens(nph, ng, A)

            for ph in (0, 1):
                with pe.Fori(0, GROUPS - 1) as g:
                    attention(ph, g)
                attention(ph, GROUPS - 1)

            def up(g, m):
                pe.wait_ge(act_done, nth(MSTEP_F4, 2, g, m - 4))
                if m == 0:
                    pe.wait_ge(xt_lo, nth(GRP, 2, g, 0))
                pe.wait_ge(e_split, m + 1)
                for k in range(KD):
                    mm = three(H[m % 4][:, :], [arena[:, m * 2 * PIECE + s * PIECE + k * P:
                                                      m * 2 * PIECE + s * PIECE + (k + 1) * P]
                                                for s in (0, 1)],
                               [XT[:, s, k, :] for s in (0, 1)], k == 0, k == KD - 1)
                mm.then_inc(f1_ps, 1)

            def down(g, m):
                pe.wait_ge(h_lo, nth(MSTEP_F4, 2, g, m))
                if m == 0:
                    pe.wait_ge(y_read, nth(GRP_F1, 2, g, -1))
                for t in range(TILES):
                    mm = three(Y[t // 2][:, (t % 2) * D:(t % 2 + 1) * D],
                               [PT[:, m % 2, s, t * P:(t + 1) * P] for s in (0, 1)],
                               [piece(m, s, 1, 0, D) for s in (0, 1)],
                               m == 0 and t % 2 == 0, m == MCH - 1, True)
                mm.then_inc(f2_ps, 1)

            def logits(g):
                pe.wait_ge(xt_lo, nth(GRP, 2, g, 0))
                for t in range(TILES):
                    for k in range(KD):
                        mm = three(T[:, t * EXPERTS:(t + 1) * EXPERTS],
                                   [XT[:, s, k, t * P:(t + 1) * P] for s in (0, 1)],
                                   [gate[:, s, k * EXPERTS:(k + 1) * EXPERTS] for s in (0, 1)],
                                   k == 0, k == KD - 1)
                mm.then_inc(lg_ps, 1)

            def experts(g):
                last = isinstance(g, int) and g == GROUPS - 1
                for m in range(MCH + 2):
                    if m < MCH:
                        up(g, m)
                    if m == 1:
                        logits(g)
                    if m == MCH and not last:
                        pe.wait_ge(lg_v, g * LGV + 1)
                        transpose_tokens(2, g + 1, (T, O))
                    if m >= 2:
                        down(g, m - 2)

            with pe.Fori(0, GROUPS - 1) as g:
                experts(g)
            experts(GROUPS - 1)

        @block.scalar
        def _(act):
            act.dma_start(bias[:, :], biases).then_inc(b_in, 16)
            act.dma_start(rowc[:, :], rows[0:1, 0:2 * D + 2 * EXPERTS].to_broadcast(
                [P, 2 * D + 2 * EXPERTS])).then_inc(b_in, 16)
            act.dma_start(b2raw, rows[0:1, 2 * D + 2 * EXPERTS:].to_broadcast(
                [P, EXPERTS * D])).then_inc(b_in, 16)
            act.dma_start(msk[:, :], mask).then_inc(b_in, 16)
            act.dma_start(gst[:, :], gateT).then_inc(b_in, 16)

            def tokens_hi(ph, g, banks):
                act.wait_ge(xt_ps, nth(GRP, ph, g, 0))
                for k in range(KD):
                    last = act.activation(XT[:, 0, k, :], banks[k][:, :], ACT.Copy)
                last.then_inc(xt_hi, 1)

            def weight_hi(i):
                act.wait_ge(w_in[i % 4], 16 * (i // 4 + 1))
                scale = (DH1 ** -0.5 if i < N1 and i % 4 == 0 else DH2 ** -0.5 if i == N1 else 1.0)
                act.activation(arena[:, i * 2 * PIECE:i * 2 * PIECE + PIECE], wst[:, i % 4, :], ACT.Copy,
                               scale=scale).then_inc(w_hi, 1)

            def qk_evac(ph, g, job):
                c, is_k = job // 2, job % 2
                act.wait_ge(qk_ps, nth(QK, ph, g, job))
                if not is_k:
                    col = (BQ1 if ph == 0 else BQ2) + c
                    last = act.activation(Q[:, c % 2, 0, :], A0[:, :], ACT.Identity,
                                          bias=bias[:, col:col + 1])
                elif ph == 0:
                    for h in range(2):
                        rows_ = slice(h * DH1, (h + 1) * DH1)
                        last = act.activation(K[rows_, c % 2, 0, :, h, :],
                                              A0[rows_, :].rearrange("p (b c) -> p b c", b=TILES),
                                              ACT.Identity, bias=bias[rows_, BK1 + c:BK1 + c + 1])
                else:
                    for h in range(2):
                        last = act.activation(K[:, c % 2, 0, :, h, :],
                                              A0[:, :].rearrange("p (b c) -> p b c", b=TILES),
                                              ACT.Identity, scale=half[:, h:h + 1],
                                              bias=bkh[:, 2 * c + h:2 * c + h + 1])
                last.then_inc(qk_hi, 1)

            def v_evac(ph, g, cp, t):
                act.wait_ge(v_ps, nth(VJ, ph, g, 4 * cp + t))
                used = 4 * (cp - 1) - 1 if ph == 0 else -1
                if t == 0 and not (ph == 0 and cp == 0 and isinstance(g, int) and g == 0):
                    act.wait_ge(pv_ps, nth(SLOT_F2, ph, g, used))
                src = A1 if ph == 0 or t % 2 == 0 else A0
                act.activation(V[:, cp % 2 if ph == 0 else 0, 0, t, :], src[:, 0:256],
                               ACT.Copy).then_inc(v_hi, 1)

            act.wait_ge(ready_v, 1)
            for i in range(3):
                weight_hi(i)
            tokens_hi(0, 0, A)
            act.wait_ge(ready, 3)
            qk_evac(0, 0, 0)
            qk_evac(0, 0, 1)
            for t in range(TILES):
                v_evac(0, 0, 0, t)
                weight_hi(3 + t)
            act.activation(gate[:, 0, :], gst[:, :], ACT.Copy).then_inc(w_hi, 1)
            for i in range(7, N1 + N2):
                weight_hi(i)

            def exp_probs(ph, g, n):
                act.wait_ge(maxed, nth(SLOT, ph, g, n))
                act.wait_ge(pt_ps, nth(SLOT_F4, ph, g, n - 4))
                for u in range(4):
                    last = act.activation(probs[:, n % 4, u * P:(u + 1) * P],
                                          S[n % 2][:, u * P:(u + 1) * P], ACT.Exp,
                                          bias=nm[:, n % 4, u:u + 1], accum_out=rsum[:, n % 4, u:u + 1])
                last.then_inc(exped, 1)

            def probs_hi(ph, g, n):
                act.wait_ge(pt_ps, nth(SLOT_F4, ph, g, n))
                act.wait_ge(pv_ps, nth(SLOT_F2, ph, g, n - 2))
                act.activation(PT[:, n % 2, 0, :], T[:, :], ACT.Copy).then_inc(pt_hi, 1)

            def out_hi(ph, g, n):
                c = n // 2
                act.wait_ge(pv_ps, nth(SLOT_F2, ph, g, n))
                if ph == 0:
                    if n % 2 == 0:
                        act.wait_ge(oproj, nth(OPROJ, ph, g, c - 2))
                    for h in range(2):
                        last = act.activation(
                            AT[h * DH1:(h + 1) * DH1, c % 2, 0, (n % 2) * 256:(n % 2 + 1) * 256]
                            .rearrange("p (b c) -> p b c", b=2),
                            O[0:DH1, :].rearrange("p (b h c) -> p b h c", b=2, h=2)[:, :, h, :],
                            ACT.Identity, bias=bias[0:DH1, BV1 + 2 * c + h:BV1 + 2 * c + h + 1])
                else:
                    if n % 8 == 0:
                        act.wait_ge(at_lo, nth(ATC_F2, ph, g, c // 4 - 2))
                    rows_ = slice(32 * (c % 4), 32 * (c % 4) + 32)
                    last = act.activation(
                        araw[rows_, c // 4, (n % 2) * 256:(n % 2 + 1) * 256]
                        .rearrange("p (b c) -> p b c", b=2),
                        O[0:32, :].rearrange("p (b h c) -> p b h c", b=2, h=2)[:, :, 0, :],
                        ACT.Copy, scale=half[0:32, 0:1])
                last.then_inc(o_hi, 1)

            def attention(ph, g):
                nph, ng = following(ph, g)
                for n in range(SLOTS):
                    if n < QUADS:
                        exp_probs(ph, g, n)
                    for job in qk_jobs(ph, n):
                        qk_evac(ph, g, job)
                    if nph < 2 and next_q(ph, n) is not None:
                        qk_evac(nph, ng, next_q(ph, n))
                    if 1 <= n <= QUADS:
                        probs_hi(ph, g, n - 1)
                    if 2 <= n <= QUADS + 1:
                        out_hi(ph, g, n - 2)
                    for t, cp in v_jobs(ph, n):
                        v_evac(ph, g, cp, t)
                    if nph < 2:
                        for t in next_v(ph, n):
                            v_evac(nph, ng, 0, t)
                    if ph == 1 and n in (10, 18):
                        cc = 0 if n == 10 else 1
                        act.wait_ge(o_lo, nth(SLOT_F1, ph, g, 8 * cc + 7))
                        act.wait_ge(oproj, nth(OPROJ, ph, g, cc - 2))
                        act.activation(AT[:, cc, 0, :], araw[:, cc, :], ACT.Identity,
                                       bias=bias[:, BV2 + cc:BV2 + cc + 1]).then_inc(at_hi, 1)
                    if nph == 1 and n == CT_SLOT:
                        act.wait_ge(c_in, nth(CTX, 1, ng, 0) * 16)
                        if ph == 1:
                            act.wait_ge(qk_ps, nth(QK, 1, g, 3))
                        for k in range(KD):
                            last = act.activation(CT[:, 0, k, :], craw[:, k * GT:(k + 1) * GT], ACT.Copy)
                        last.then_inc(c_hi, 1)
                    if n == XT_SLOT[ph]:
                        tokens_hi(nph, ng, A)

            for ph in (0, 1):
                with act.Fori(0, GROUPS - 1) as g:
                    attention(ph, g)
                attention(ph, GROUPS - 1)

            def experts(g):
                last = isinstance(g, int) and g == GROUPS - 1
                for m in range(MCH):
                    act.wait_ge(f1_ps, nth(MSTEP, 2, g, m))
                    act.wait_ge(h_lo, nth(MSTEP_F4, 2, g, m - 4))
                    act.activation(probs[:, m % 4, :], H[m % 4][:, :], ACT.Gelu,
                                   bias=bias[:, B1 + m:B1 + m + 1]).then_inc(act_done, 1)
                    act.wait_ge(act_done, nth(MSTEP_F4, 2, g, m))
                    act.wait_ge(f2_ps, nth(MSTEP_F2, 2, g, m - 2))
                    act.activation(PT[:, m % 2, 0, :], probs[:, m % 4, :], ACT.Copy).then_inc(h_hi, 1)
                    if m == 12:
                        act.wait_ge(lg_v, g * LGV + 8)
                        act.activation(lg[:, 4, :], lg[:, 3, :], ACT.Exp, scale=2.0).then_inc(lg_exp, 1)
                if not last:
                    tokens_hi(2, g + 1, (T, O))

            with act.Fori(0, GROUPS - 1) as g:
                experts(g)
            experts(GROUPS - 1)


        @block.vector
        def _(dve):
            def sub_lo(out_, src, hi, sem_):
                dve.tensor_tensor(out_, src, hi.bitcast(F32), ALU.subtract).then_inc(sem_, 1)

            def ln_stats(ph, g, t):
                tile_ = (g * TILES + t)
                dve.bn_stats(st[:, t, :], xs[:, tile_, :] if isinstance(tile_, int) else
                             xs[:, bass.ds(tile_, 1), :].rearrange("p a d -> p (a d)")
                             ).then_inc(ln_stat, 1)

            def ln_finish(ph, g):
                dve.wait_ge(ln_stat, nth(LNST, ph, g, TILES - 1))
                dve.sem_inc(dve_gate, 1)
                for t in range(TILES):
                    last = dve.bn_aggr(mv[:, t, :], st[:, t, :])
                last.then_inc(ln_aggr, 1)
                dve.wait_ge(ln_aggr, nth(GRP, ph, g, 0))
                dve.tensor_scalar(ve[:, :], mv[:, :, 1], LN_EPS, None, ALU.add).then_inc(ln_var, 1)

            def ln_apply(ph, g):
                dve.wait_ge(ln_rstd, nth(GRP, ph, g, 0))
                if not (ph == 0 and isinstance(g, int) and g == 0):
                    dve.wait_ge(xt_ps, nth(GRP, ph, g, -1))
                for t in range(TILES):
                    tile_ = g * TILES + t
                    src = xs[:, tile_, :] if isinstance(tile_, int) else \
                        xs[:, bass.ds(tile_, 1), :].rearrange("p a d -> p (a d)")
                    last = dve.tensor_scalar(xn[:, t, :], src, mv[:, t, 0:1], rstd[:, t:t + 1],
                                             ALU.subtract, ALU.mult)
                last.then_inc(ln_x, 1)

            def tokens_lo(ph, g, banks):
                dve.wait_ge(xt_hi, nth(GRP, ph, g, 0))
                for k in range(KD):
                    last = dve.tensor_tensor(XT[:, 1, k, :], banks[k][:, :], XT[:, 0, k, :].bitcast(F32),
                                             ALU.subtract)
                last.then_inc(xt_lo, 1)

            def weight_lo(i):
                dve.wait_ge(w_hi, i + 1 + (i >= 7))
                scale = (DH1 ** -0.5 if i < N1 and i % 4 == 0 else DH2 ** -0.5 if i == N1 else 1.0)
                at = i * 2 * PIECE
                dve.scalar_tensor_tensor(arena[:, at + PIECE:at + 2 * PIECE], wst[:, i % 4, :], scale,
                                         arena[:, at:at + PIECE].bitcast(F32), ALU.mult,
                                         ALU.subtract).then_inc(w_split, 1)

            def qk_low(ph, g, job):
                c, is_k = job // 2, job % 2
                dve.wait_ge(qk_hi, nth(QK, ph, g, job))
                if not is_k:
                    col = (BQ1 if ph == 0 else BQ2) + c
                    last = dve.scalar_tensor_tensor(Q[:, c % 2, 1, :], A0[:, :], bias[:, col:col + 1],
                                                    Q[:, c % 2, 0, :].bitcast(F32), ALU.add, ALU.subtract)
                elif ph == 0:
                    for h in range(2):
                        rows_ = slice(h * DH1, (h + 1) * DH1)
                        last = dve.scalar_tensor_tensor(
                            K[rows_, c % 2, 1, :, h, :],
                            A0[rows_, :].rearrange("p (b c) -> p b c", b=TILES),
                            bias[rows_, BK1 + c:BK1 + c + 1],
                            K[rows_, c % 2, 0, :, h, :].bitcast(F32), ALU.add, ALU.subtract)
                else:
                    dve.tensor_scalar(A0[:, :], A0[:, :], bias[:, BK2 + c:BK2 + c + 1], None,
                                      ALU.add).then_inc(kbias, 1)
                    dve.wait_ge(kbias, nth(ATC, 1, g, c))
                    for h in range(2):
                        last = dve.scalar_tensor_tensor(
                            K[:, c % 2, 1, :, h, :], A0[:, :].rearrange("p (b c) -> p b c", b=TILES),
                            half[:, h:h + 1], K[:, c % 2, 0, :, h, :].bitcast(F32),
                            ALU.mult, ALU.subtract)
                last.then_inc(qk_lo, 1)

            def v_low(ph, g, cp, t):
                dve.wait_ge(v_hi, nth(VJ, ph, g, 4 * cp + t))
                r = cp % 2 if ph == 0 else 0
                src = A1 if ph == 0 or t % 2 == 0 else A0
                sub_lo(V[:, r, 1, t, :], src[:, 0:256], V[:, r, 0, t, :], v_lo)

            dve.wait_ge(b_in, 80)
            dve.wait_ge(ready, 2)
            for h in range(2):
                dve.tensor_reduce(half[:, h:h + 1],
                                  ident[:, :].rearrange("p (a h c) -> p a h c", a=4, h=2)[:, :, h, :],
                                  axis=AX.XY, op=ALU.add).then_inc(dve_gate, 1)
            dve.tensor_scalar(bias[:, BQ1:BQ1 + 8], bias[:, BQ1:BQ1 + 8], DH1 ** -0.5, None, ALU.mult)
            dve.tensor_scalar(bias[:, BQ2:BQ2 + 2], bias[:, BQ2:BQ2 + 2], DH2 ** -0.5, None, ALU.mult)
            dve.tensor_scalar(dropped[:, :], msk[:, :], 0.0, None, ALU.is_equal)
            dve.memset(neg[:, :], MASKED)
            dve.memset(mhalf[:, :], -0.5)
            dve.tensor_reduce(b2sum[:, :], b2raw.rearrange("p (e d) -> p d e", e=EXPERTS),
                              axis=AX.X, op=ALU.add)
            dve.wait_ge(dve_gate, 2)
            for c in range(2):
                for h in range(2):
                    last = dve.tensor_tensor(bkh[:, 2 * c + h:2 * c + h + 1], bias[:, BK2 + c:BK2 + c + 1],
                                             half[:, h:h + 1], ALU.mult)
            last.then_inc(ready_v, 1)

            dve.wait_ge(x_in, GROUPS * 16)
            for t in range(TILES):
                ln_stats(0, 0, t)
            ln_finish(0, 0)
            ln_apply(0, 0)
            for i in range(3):
                weight_lo(i)
            tokens_lo(0, 0, A)
            dve.wait_ge(ready, 3)
            qk_low(0, 0, 0)
            qk_low(0, 0, 1)
            for t in range(TILES):
                v_low(0, 0, 0, t)
                weight_lo(3 + t)
            dve.wait_ge(w_hi, 8)
            sub_lo(gate[:, 1, :], gst[:, :], gate[:, 0, :], dve_gate)
            for i in range(7, N1 + N2):
                weight_lo(i)

            def row_max(ph, g, n):
                dve.wait_ge(scores_ps, nth(SLOT, ph, g, n))
                s3 = S[n % 2][:, :].rearrange("p (u c) -> p u c", u=4)
                if ph == 1:
                    dve.sem_inc(dve_gate, 1)
                    dve.copy_predicated(s3, dropped[:, :].unsqueeze(1).to_broadcast([P, 4, P]),
                                        neg[:, :].unsqueeze(2).to_broadcast([P, 4, P])
                                        ).then_inc(filled, 1)
                    dve.wait_ge(filled, g * QUADS + n + 1)
                dve.tensor_reduce(nm[:, n % 4, :], s3, axis=AX.X, op=ALU.max, negate=True
                                  ).then_inc(maxed, 1)

            def row_inverse(ph, g, n):
                dve.wait_ge(exped, nth(SLOT_F2, ph, g, n))
                dve.reciprocal(rinv[:, n % 4, :], rsum[:, n % 4, :]).then_inc(inverted, 1)

            def probs_low(ph, g, n):
                dve.wait_ge(pt_hi, nth(SLOT, ph, g, n))
                sub_lo(PT[:, n % 2, 1, :], T[:, :], PT[:, n % 2, 0, :], pt_lo)

            def out_low(ph, g, n):
                c = n // 2
                dve.wait_ge(o_hi, nth(SLOT, ph, g, n))
                o4 = O[:, :].rearrange("p (b h c) -> p b h c", b=2, h=2)
                cols = slice((n % 2) * 256, (n % 2 + 1) * 256)
                if ph == 0:
                    for h in range(2):
                        rows_ = slice(h * DH1, (h + 1) * DH1)
                        last = dve.scalar_tensor_tensor(
                            AT[rows_, c % 2, 1, cols].rearrange("p (b c) -> p b c", b=2),
                            o4[0:DH1, :, h, :], bias[0:DH1, BV1 + 2 * c + h:BV1 + 2 * c + h + 1],
                            AT[rows_, c % 2, 0, cols].rearrange("p (b c) -> p b c", b=2).bitcast(F32),
                            ALU.add, ALU.subtract)
                else:
                    rows_ = slice(32 * (c % 4), 32 * (c % 4) + 32)
                    dst = araw[rows_, c // 4, cols].rearrange("p (b c) -> p b c", b=2)
                    last = dve.scalar_tensor_tensor(dst, o4[0:32, :, 1, :], half[0:32, 1:2], dst,
                                                    ALU.mult, ALU.add)
                last.then_inc(o_lo, 1)

            def add_residual(ph, g):
                dve.wait_ge(oproj, nth(OPROJ, ph, g, OPROJ.per[ph] - 1))
                for j in range(2):
                    at = g * TILES + 2 * j
                    dst = xs[:, bass.ds(at, 2), :] if not isinstance(at, int) else xs[:, at:at + 2, :]
                    last = dve.tensor_tensor(dst, Y[j][:, :].rearrange("p (t d) -> p t d", t=2), dst,
                                             ALU.add)
                last.then_inc(y_read, 1)

            def attention(ph, g):
                nph, ng = following(ph, g)
                ln0 = 8 if ph == 0 else 2
                for n in range(SLOTS):
                    if n < QUADS:
                        row_max(ph, g, n)
                    if 3 <= n <= QUADS + 2:
                        out_low(ph, g, n - 3)
                    for t, cp in v_jobs(ph, n - 1):
                        v_low(ph, g, cp, t)
                    if nph < 2:
                        for t in next_v(ph, n - 1):
                            v_low(nph, ng, 0, t)
                    if n < QUADS:
                        row_inverse(ph, g, n)
                    for job in qk_jobs(ph, n):
                        qk_low(ph, g, job)
                    if nph < 2 and next_q(ph, n) is not None:
                        qk_low(nph, ng, next_q(ph, n))
                    if 1 <= n <= QUADS:
                        probs_low(ph, g, n - 1)
                    if ph == 1 and n in (10, 18):
                        cc = 0 if n == 10 else 1
                        dve.wait_ge(at_hi, nth(ATC, ph, g, cc))
                        dve.scalar_tensor_tensor(AT[:, cc, 1, :], araw[:, cc, :],
                                                 bias[:, BV2 + cc:BV2 + cc + 1],
                                                 AT[:, cc, 0, :].bitcast(F32), ALU.add,
                                                 ALU.subtract).then_inc(at_lo, 1)
                    if ln0 <= n < ln0 + TILES:
                        if n == ln0 and nph > 0:
                            dve.wait_ge(x_ready, nth(GRP, nph - 1, ng, 0))
                            dve.sem_inc(dve_gate, 1)
                        ln_stats(nph, ng, n - ln0)
                    if n == ln0 + TILES:
                        ln_finish(nph, ng)
                    if n == ln0 + TILES + 1:
                        ln_apply(nph, ng)
                    if nph == 1 and n == CT_SLOT:
                        dve.wait_ge(c_hi, nth(CTX, 1, ng, 0))
                        for k in range(KD):
                            last = dve.tensor_tensor(CT[:, 1, k, :], craw[:, k * GT:(k + 1) * GT],
                                                     CT[:, 0, k, :].bitcast(F32), ALU.subtract)
                        last.then_inc(c_lo, 1)
                    if n == XT_SLOT[ph]:
                        tokens_lo(nph, ng, A)
                if nph < 2:
                    for t in next_v(ph, SLOTS - 1):
                        v_low(nph, ng, 0, t)
                add_residual(ph, g)

            for ph in (0, 1):
                with dve.Fori(0, GROUPS - 1) as g:
                    attention(ph, g)
                attention(ph, GROUPS - 1)

            def gating(g, step):
                def after(n):
                    dve.wait_ge(lg_v, g * LGV + n)

                def l3(i):
                    return lg[:, i, :].rearrange("p (t e) -> p t e", t=TILES)

                def row(i):
                    return rowc[:, 2 * D + i * EXPERTS:2 * D + (i + 1) * EXPERTS].unsqueeze(1) \
                        .to_broadcast([P, TILES, EXPERTS])

                def col(i):
                    return gs[:, i, :].unsqueeze(2).to_broadcast([P, TILES, EXPERTS])

                if step == 0:
                    dve.wait_ge(lg_ps, g + 1)
                    dve.tensor_tensor(l3(0), T[:, 0:TILES * EXPERTS].rearrange("p (t e) -> p t e", t=TILES),
                                      row(0), ALU.add).then_inc(lg_v, 1)
                elif step == 1:
                    after(1)
                    dve.tensor_tensor(lg[:, 1, :], lg[:, 0, :], lg[:, 0, :], ALU.mult).then_inc(lg_v, 1)
                elif step == 2:
                    after(2)
                    dve.tensor_reduce(gs[:, 0, :], l3(1), axis=AX.X, op=ALU.add).then_inc(lg_v, 1)
                elif step == 3:
                    after(3)
                    dve.tensor_scalar(gs[:, 1, :], gs[:, 0, :], 1.0 / EXPERTS, F32_EPS, ALU.mult,
                                      ALU.add).then_inc(lg_v, 1)
                elif step == 4:
                    dve.wait_ge(lg_pow, g + 1)
                    dve.tensor_tensor(l3(1), l3(0), col(2), ALU.mult).then_inc(lg_v, 1)
                elif step == 5:
                    after(5)
                    dve.tensor_tensor(l3(2), l3(1), row(1), ALU.mult).then_inc(lg_v, 1)
                elif step == 6:
                    after(6)
                    dve.tensor_reduce(gs[:, 3, :], l3(2), axis=AX.X, op=ALU.max).then_inc(lg_v, 1)
                elif step == 7:
                    after(7)
                    dve.tensor_tensor(l3(3), l3(2), col(3), ALU.subtract).then_inc(lg_v, 1)
                elif step == 8:
                    dve.wait_ge(lg_exp, g + 1)
                    dve.tensor_reduce(gs[:, 4, :], l3(4), axis=AX.X, op=ALU.add).then_inc(lg_v, 1)
                elif step == 9:
                    after(9)
                    dve.reciprocal(gs[:, 5, :], gs[:, 4, :]).then_inc(lg_v, 1)
                elif step == 10:
                    after(10)
                    dve.tensor_scalar(gs[:, 6, :], gs[:, 5, :], 1e-6, None, ALU.add).then_inc(lg_v, 1)
                elif step == 11:
                    after(11)
                    dve.reciprocal(gs[:, 3, :], gs[:, 6, :]).then_inc(lg_v, 1)
                elif step == 12:
                    after(12)
                    dve.tensor_tensor(gs[:, 7, :], gs[:, 5, :], gs[:, 3, :], ALU.mult).then_inc(ng_done, 1)

            def finish(g):
                dve.wait_ge(f2_ps, nth(MSTEP_F2, 2, g, MCH - 1))
                if not (isinstance(g, int) and g == 0):
                    dve.wait_ge(out_dma, g * 16)
                for j in range(2):
                    last = dve.tensor_tensor(yo[:, 2 * j:2 * j + 2, :],
                                             Y[j][:, :].rearrange("p (t d) -> p t d", t=2),
                                             b2sum[:, :].unsqueeze(1).to_broadcast([P, 2, D]), ALU.add)
                last.then_inc(y_read, 1)
                dve.wait_ge(y_read, nth(GRP_F1, 2, g, 0))
                dve.wait_ge(ng_done, g + 1)
                for t in range(TILES):
                    at = g * TILES + t
                    src = xs[:, at, :] if isinstance(at, int) else \
                        xs[:, bass.ds(at, 1), :].rearrange("p a d -> p (a d)")
                    last = dve.scalar_tensor_tensor(yo[:, t, :], yo[:, t, :], gs[:, 7, t:t + 1], src,
                                                    ALU.mult, ALU.add)
                last.then_inc(fin, 1)

            def experts(g):
                last = isinstance(g, int) and g == GROUPS - 1
                for m in range(MCH):
                    dve.wait_ge(h_hi, nth(MSTEP, 2, g, m))
                    sub_lo(PT[:, m % 2, 1, :], probs[:, m % 4, :], PT[:, m % 2, 0, :], h_lo)
                    if 4 <= m <= 11:
                        gating(g, m - 4)
                    if 14 <= m <= 18:
                        gating(g, m - 6)
                    if not last:
                        if 20 <= m < 24:
                            if m == 20:
                                dve.wait_ge(x_ready, nth(GRP, 1, g + 1, 0))
                                dve.sem_inc(dve_gate, 1)
                            ln_stats(2, g + 1, m - 20)
                        if m == 24:
                            ln_finish(2, g + 1)
                        if m == 28:
                            ln_apply(2, g + 1)
                if not last:
                    tokens_lo(2, g + 1, (T, O))
                finish(g)

            experts(0)
            with dve.Fori(1, GROUPS - 1) as g:
                experts(g)
            experts(GROUPS - 1)

        @block.gpsimd
        def _(pool):
            for s, c in ((pt_ps, 4), (exped, 2), (pv_ps, 2), (pt_lo, 1), (o_lo, 1), (oproj, 2),
                         (qk_lo, 1), (v_lo, 2), (y_read, 1), (act_done, 4), (h_lo, 4), (f2_ps, 2), (at_lo, 2)):
                pool.sem_inc(s, c)
            pool.memset(ident[:, :], 0.0).then_inc(ready, 1)
            pool.wait_ge(ready, 1)
            pool.affine_select(out=ident[:, :], in_=ident[:, :], compare_op=ALU.not_equal, fill=1.0,
                               base=0, pattern=[[-1, P]], channel_multiplier=1).then_inc(ready, 1)
            pool.memset(K.rearrange("p r s b h c -> p (r s b h c)").bitcast(F32), 0.0).then_inc(ready, 1)

            def inv_sqrt(ph, g):
                pool.wait_ge(ln_var, nth(GRP, ph, g, 0))
                pool.tensor_tensor(rstd[:, :], ve[:, :], mhalf[:, :], ALU.pow).then_inc(ln_rstd, 1)

            inv_sqrt(0, 0)

            def normalise(ph, g, n):
                pool.wait_ge(inverted, nth(SLOT, ph, g, n))
                p3 = probs[:, n % 4, :].rearrange("p (u c) -> p u c", u=4)
                pool.tensor_tensor(p3, p3, rinv[:, n % 4, :].unsqueeze(2).to_broadcast([P, 4, P]),
                                   ALU.mult).then_inc(normed, 1)

            def split_expert(g, j):
                loads = (N1 + N2) // 4
                pool.wait_ge(w_in[j], (g + loads + 1) * 16)
                pool.sem_inc(pool_gate, 1)
                at = (g * 4 + j) * (2 * PIECE)
                if isinstance(at, int):
                    hi, lo = arena[:, at:at + PIECE], arena[:, at + PIECE:at + 2 * PIECE]
                else:
                    hi, lo = arena[:, bass.ds(at, PIECE)], arena[:, bass.ds(at + PIECE, PIECE)]
                pool.tensor_copy(hi, wst[:, j, :]).then_inc(e_hi, 1)
                pool.wait_ge(e_hi, g * 4 + j + 1)
                pool.sem_inc(pool_gate, 1)
                pool.tensor_tensor(lo, wst[:, j, :], hi.bitcast(F32), ALU.subtract).then_inc(e_split, 1)

            def attention(ph, g):
                nph, ng = following(ph, g)
                ln0 = 8 if ph == 0 else 2
                for n in range(QUADS):
                    normalise(ph, g, n)
                    if n == ln0 + TILES:
                        inv_sqrt(nph, ng)
                    if ph == 1 and n % 4 == 3:
                        split_expert(g, n // 4)
                pool.wait_ge(y_read, nth(GRP_F1, ph, g, 0))
                pool.sem_inc(pool_gate, 1)
                at = g * TILES
                dst = xs[:, at:at + TILES, :] if isinstance(at, int) else xs[:, bass.ds(at, TILES), :]
                pool.tensor_tensor(dst, dst, rowc[:, ph * D:(ph + 1) * D].unsqueeze(1)
                                   .to_broadcast([P, TILES, D]), ALU.add).then_inc(x_ready, 1)

            for ph in (0, 1):
                with pool.Fori(0, GROUPS - 1) as g:
                    attention(ph, g)
                attention(ph, GROUPS - 1)
                if ph == 0:
                    pool.wait_ge(oproj, nth(OPROJ, 0, GROUPS - 1, CHUNKS1 - 1))

            def inv_rms(g):
                pool.wait_ge(lg_v, g * LGV + 4)
                pool.tensor_tensor(gs[:, 2, :], gs[:, 1, :], mhalf[:, :], ALU.pow).then_inc(lg_pow, 1)

            pool.wait_ge(oproj, nth(OPROJ, 1, GROUPS - 1, 1))
            for j in range(4):
                split_expert(GROUPS, j)
            inv_rms(0)
            with pool.Fori(GROUPS + 1, 2 * GROUPS) as g:
                for j in range(4):
                    split_expert(g, j)
            inv_sqrt(2, 1)
            with pool.Fori(1, GROUPS - 1) as g:
                inv_rms(g)
                inv_sqrt(2, g + 1)
            inv_rms(GROUPS - 1)


_OUT = (16, 128, 256)


def kernel(**inputs):
    import numpy as np
    import concourse.bacc as bacc
    from concourse.bass_utils import run_bass_kernel_spmd as run

    f = {k: np.asarray(v) for k, v in inputs.items()}

    def halves(w):
        n = w.shape[1] // 256
        return w.reshape(2, P, n, 256).transpose(2, 1, 0, 3).reshape(n, P, PIECE)

    wq, wk, wv = (halves(f["L0_attn_W_" + c].reshape(HEADS * DH1, D).T) for c in "QKV")
    wo = f["L0_attn_W_O"].transpose(0, 2, 1).reshape(4, 2, P, D).transpose(0, 2, 1, 3).reshape(4, P, PIECE)
    first = np.stack([wq, wk, wv, wo], axis=1).reshape(N1, P, PIECE)
    second = np.concatenate([halves(f["L0_xattn_W" + c].T) for c in "qkvo"])
    w1 = f["L0_ffn_w1"].transpose(1, 0, 2).reshape(KD, P, MCH, P).transpose(2, 1, 0, 3).reshape(MCH, P, 256)
    w2 = f["L0_ffn_w2"].reshape(MCH, P, D)
    pieces = np.concatenate([first, second, np.concatenate([w1, w2], axis=2)])

    bv1 = np.concatenate([f["L0_attn_b_V"].reshape(HEADS, DH1).T] * 2)
    biases = np.concatenate(
        [f["L0_attn_b_Q"].reshape(8, P).T, f["L0_attn_b_K"].reshape(8, P).T, bv1]
        + [f["L0_xattn_b" + c].reshape(2, P).T for c in "qkv"] + [f["L0_ffn_b1"].reshape(MCH, P).T], axis=1)
    rows = np.concatenate([f["L0_attn_b_O"], f["L0_xattn_bo"], f["L0_ffn_gate_b"], f["L0_ffn_rms_w"],
                           f["L0_ffn_b2"].reshape(-1)]).reshape(1, -1)
    gateT = f["L0_ffn_gate_w"].T.reshape(KD, P, EXPERTS).transpose(1, 0, 2).reshape(P, KD * EXPERTS)
    x = f["x"].reshape(GROUPS, TILES, P, D).transpose(0, 2, 1, 3)
    ctxT = f["ctx_1024"].reshape(GROUPS, GT, KD, P).transpose(0, 3, 2, 1)
    mask = f["mask_1x1xSxS2_bk0"].reshape(P, P)

    nc = bacc.Bacc("TRN2", target_bir_lowering=False, num_devices=1)
    arrays, args = {}, []
    for name, a in (("x", x), ("ctxT", ctxT), ("mask", mask), ("pieces", pieces), ("gateT", gateT),
                    ("biases", biases), ("rows", rows)):
        a = np.ascontiguousarray(a)
        arrays["in_" + name] = a
        args.append(nc.dram_tensor("in_" + name, a.shape, mybir.dt.from_np(a.dtype),
                                   kind="ExternalInput").ap())
    args.append(nc.dram_tensor("out_0", (GROUPS, P, TILES, D), F32, kind="ExternalOutput").ap())
    build(nc, *args)
    got = run(nc, [arrays], core_ids=[0]).results[0]["out_0"]
    return got.transpose(0, 2, 1, 3).reshape(_OUT)
```

```python
from collections import namedtuple
from contextlib import ExitStack

import concourse.bass as bass
from concourse import mybir

F32 = mybir.dt.float32
F32R = mybir.dt.float32r
U8 = mybir.dt.uint8
ALU = mybir.AluOpType
ACT = mybir.ActivationFunctionType
AX = mybir.AxisListType

P = 128
D = 256
KD = D // P
GROUPS = 4
TILES = 4
GT = TILES * P
QUADS = 16
PERIOD = QUADS
HEADS = 16
DH1, DH2 = 64, 16
CHUNKS1 = HEADS * DH1 // P
EXPERTS, HID = 8, 512
MCH = EXPERTS * HID // P
PIECE = 512
N1, N2 = 16, 4
LN_EPS = 1e-5
F32_EPS = 1.1920928955078125e-07
MASKED = -1e9

BQ1, BK1, BV1 = 0, 8, 16
BQ2, BK2, BV2, B1 = 32, 34, 36, 38
NBIAS = B1 + MCH

Count = namedtuple("Count", "credit per")


def nth(count, ph, g, i):
    return count.credit + GROUPS * sum(count.per[:ph]) + g * count.per[ph] + i + 1


SLOT = Count(0, (16, 16, 0))
SLOT_F1 = Count(1, (16, 16, 0))
SLOT_F2 = Count(2, (16, 16, 0))
SLOT_F4 = Count(4, (16, 16, 0))
QK = Count(0, (16, 4, 0))
QK_F1 = Count(1, (16, 4, 0))
VJ = Count(0, (16, 2, 0))
VJ_F1 = Count(1, (16, 2, 0))
ATC = Count(0, (0, 2, 0))
ATC_F2 = Count(2, (0, 2, 0))
OPROJ = Count(2, (8, 2, 0))
GRP = Count(0, (1, 1, 1))
GRP_F1 = Count(1, (1, 1, 1))
CTX = Count(0, (0, 1, 0))
MSTEP = Count(0, (0, 0, MCH))
MSTEP_F2 = Count(2, (0, 0, MCH))
MSTEP_F4 = Count(4, (0, 0, MCH))
LNST = Count(0, (TILES, TILES, TILES))


def build(nc, x, ctxT, mask, pieces, gateT, biases, rows, out):
    with ExitStack() as ctx:
        def sb(name, shape, dt):
            return ctx.enter_context(nc.sbuf_tensor(name, shape, dt))

        def bank(name):
            return ctx.enter_context(nc.psum_tensor(name, [P, 512], F32))

        def sem(name):
            return ctx.enter_context(nc.semaphore(name))

        arena = sb("arena", [P, MCH * 2 * PIECE], F32R)
        work = (N1 + N2) * 2 * PIECE

        def piece(i, lo, k, a, b):
            at = i * 2 * PIECE + lo * PIECE + k * 256
            return arena[:, at + a:at + b]

        def region(cols):
            nonlocal work
            at = work
            work += cols
            return arena[:, at:at + cols]

        V = region(4096).rearrange("p (r s t c) -> p r s t c", r=2, s=2, t=TILES)
        K = region(4096).rearrange("p (r s b h c) -> p r s b h c", r=2, s=2, b=TILES, h=2)
        Q = region(2048).rearrange("p (r s c) -> p r s c", r=2, s=2)
        AT = region(2048).rearrange("p (r s c) -> p r s c", r=2, s=2)
        assert work == MCH * 2 * PIECE

        PT = sb("PT", [P, 2, 2, 512], F32R)
        XT = sb("XT", [P, 2, KD, GT], F32R)
        CT = sb("CT", [P, 2, KD, GT], F32R)
        gate = sb("gate", [P, KD, 2, EXPERTS], F32R)
        probs = sb("probs", [P, 4, 512], F32)
        xs = sb("xs", [P, GROUPS * TILES, D], F32)
        xn = sb("xn", [P, TILES, D], F32)
        craw = sb("craw", [P, KD * GT], F32)
        yo = craw[:, :].rearrange("p (t d) -> p t d", t=TILES)
        wst = sb("wst", [P, 4, PIECE], F32)
        araw = sb("araw", [P, 2, GT], F32)
        ident = sb("ident", [P, P], F32)
        bias = sb("bias", [P, NBIAS], F32)
        rowc = sb("rowc", [P, 2 * D + 2 * EXPERTS], F32)
        b2sum = sb("b2sum", [P, D], F32)
        gst = sb("gst", [P, KD * EXPERTS], F32)
        msk = sb("msk", [P, P], U8)
        dropped = sb("dropped", [P, P], U8)
        neg = sb("neg", [P, 1], F32)
        half = sb("half", [P, 2], F32)
        bkh = sb("bkh", [P, 4], F32)
        mhalf = sb("mhalf", [P, TILES], F32)
        nm = sb("nm", [P, 4, 4], F32)
        rsum = sb("rsum", [P, 4, 4], F32)
        rinv = sb("rinv", [P, 4, 4], F32)
        st = sb("st", [P, TILES, 6], F32)
        mv = sb("mv", [P, TILES, 2], F32)
        ve = sb("ve", [P, TILES], F32)
        rstd = sb("rstd", [P, TILES], F32)
        lg = sb("lg", [P, 5, TILES * EXPERTS], F32)
        gs = sb("gs", [P, 8, TILES], F32)
        b2raw = probs[:, :, :].rearrange("p r c -> p (r c)")

        A0, A1, S0, S1, T, O, Y0, Y1 = (bank(n) for n in ("A0", "A1", "S0", "S1", "T", "O", "Y0", "Y1"))
        A, S, Y = (A0, A1), (S0, S1), (Y0, Y1)
        H = (S0, S1, A0, A1)

        x_in = [sem("x_in0"), sem("x_in")]
        b_in = sem("b_in")
        b2_in = sem("b2_in")
        b2_sum = sem("b2_sum")
        c_in = sem("c_in")
        w_in = [sem(f"w_in{i}") for i in range(4)]
        out_dma = sem("out_dma")
        ready = sem("ready")
        ready_v = sem("ready_v")
        w_hi = sem("w_hi")
        w_split = sem("w_split")
        e_hi = sem("e_hi")
        e_split = sem("e_split")
        scores_ps = sem("scores_ps")
        filled = sem("filled")
        maxed = sem("maxed")
        exped = sem("exped")
        inverted = sem("inverted")
        normed = sem("normed")
        pt_ps = sem("pt_ps")
        pt_hi = sem("pt_hi")
        pt_lo = sem("pt_lo")
        pv_ps = sem("pv_ps")
        o_hi = sem("o_hi")
        o_lo = sem("o_lo")
        at_hi = sem("at_hi")
        at_lo = sem("at_lo")
        oproj = sem("oproj")
        qk_ps = sem("qk_ps")
        qk_hi = sem("qk_hi")
        qk_lo = sem("qk_lo")
        v_ps = sem("v_ps")
        v_hi = sem("v_hi")
        v_lo = sem("v_lo")
        xt_ps = sem("xt_ps")
        xt_hi = sem("xt_hi")
        xt_lo = sem("xt_lo")
        c_hi = sem("c_hi")
        c_lo = sem("c_lo")
        y_read = sem("y_read")
        x_ready = sem("x_ready")
        ln_stat = sem("ln_stat")
        ln_aggr = sem("ln_aggr")
        ln_var = sem("ln_var")
        ln_rstd = sem("ln_rstd")
        ln_x = sem("ln_x")
        f1_ps = sem("f1_ps")
        act_done = sem("act_done")
        h_hi = sem("h_hi")
        h_lo = sem("h_lo")
        f2_ps = sem("f2_ps")
        lg_ps = sem("lg_ps")
        lg_v = sem("lg_v")
        lg_a = sem("lg_a")
        lg_pow = sem("lg_pow")
        lg_exp = sem("lg_exp")
        y_sum = sem("y_sum")
        fin = sem("fin")
        half_built = sem("half_built")
        kbias = sem("kbias")
        ng_done = sem("ng_done")
        pe_gate = sem("pe_gate")
        dve_gate = sem("dve_gate")
        pool_gate = sem("pool_gate")
        LGV = 12

        XT_AT = 3
        SCORES = XT_AT + 4

        def steps(name, ph, v, lag=0):
            v -= lag
            if name == "quad":
                q = v - SCORES
                return [(q,)] if 0 <= q < QUADS else []
            if name == "qk":
                jobs = {XT_AT + 1 + j: j for j in range(16)} if ph == 0 else \
                    {XT_AT + 1: 0, XT_AT + 2: 1, XT_AT + 6: 2, XT_AT + 7: 3}
                return [(jobs[v],)] if v in jobs else []
            if name == "v":
                j = v - XT_AT - 1
                if ph == 0:
                    return [(j, 2)] if 0 <= j < 16 else []
                jobs = {2: (0, 0), 3: (0, 1), 7: (1, 0), 8: (1, 1)}
                return [jobs[j]] if j in jobs else []
            if name in ("qk_out", "v_out", "qk_last", "v_last"):
                own = name.endswith("last")
                done = [j[0] for j in steps(name.split("_")[0], ph, v if own else v - 1) if j[-1] or name[0] == "q"]
                return [(j,) for j in done if own == (ph == 0 and j == 15)]
            if name == "proj":
                q = v - SCORES
                if ph == 0:
                    return [(q // 2, (2 * (q % 2), 2 * (q % 2) + 1))] if 0 <= q < QUADS else []
                return {8: [(0, (0, 1))], 9: [(0, (2, 3))], 16: [(1, (0, 1))],
                        17: [(1, (2, 3))]}.get(q, [])
            if name == "outs":
                return {8: [(0,)], 16: [(1,)]}.get(v - SCORES, []) if ph == 1 else []
            if name == "residual":
                return [()] if v - SCORES == (QUADS - 1 if ph == 0 else QUADS + 1) else []
            if name == "bias":
                v -= SCORES + (QUADS if ph == 0 else QUADS + 1)
                return [(v,)] if 0 <= v < 2 else []
            if name == "stats":
                return [()] if v == 0 else []
            if name == "aggr":
                return [()] if v == 1 else []
            if name == "norm":
                return [()] if v == 2 else []
            if name == "xt":
                return [()] if v == XT_AT else []
            if name == "ctx":
                return [(v,)] if ph == 1 and 0 <= v < 4 else []
            raise ValueError(name)

        def run(order, does, ph, g, before, slots=PERIOD):
            for n in range(slots):
                for name, what, lags in order[before[0] if before and n < TURN else min(ph, 1)]:
                    for p, gg, v in ([(*before, n + PERIOD)] if before else []) + [(ph, g, n)]:
                        if p < 2 or name in ("stats", "aggr", "norm", "xt"):
                            for args in steps(what, p, v, lags[min(p, 1)]):
                                does[name](p, gg, *args)
                if name_extra := does.get("slot"):
                    name_extra(ph, g, n)

        def attentions(eng, order, does):
            run(order, does, 0, 0, None)
            with eng.Fori(1, GROUPS) as g:
                run(order, does, 0, g, (0, g - 1))
            run(order, does, 1, 0, (0, GROUPS - 1))
            with eng.Fori(1, GROUPS) as g:
                run(order, does, 1, g, (1, g - 1))
            run(order, does, 2, 0, (1, GROUPS - 1), DRAIN)

        DRAIN = 16
        TURN = 8
        LEAD = 4

        def v2(lo, job):
            return V[:, 0, lo, :, :].rearrange("p t c -> p (t c)")[:, job * 512:(job + 1) * 512]

        def w_order(i):
            return [j for n in range(PERIOD) for j in weight_slots(n)].index(i) + 1

        def w_piece(j):
            return [i for n in range(PERIOD) for i in weight_slots(n)][j]

        def weight_slots(n):
            return {2: (0, 1, 2), 3: (3,), 4: (4,), 12: (12, 16), 13: (13, 17), 14: (14, 18),
                    15: (15, 19)}.get(n, (n,) if 5 <= n < 12 else ())

        PE_ORDER = (
            (("scores", "quad", (0, 0)), ("proj", "proj", (4, 6)), ("pv", "quad", (2, 4)),
             ("transpose", "quad", (1, 3)), ("v", "v", (0, 0)), ("qk", "qk", (0, 0)),
             ("xt", "xt", (0, 0))),
            (("transpose", "quad", (1, 3)), ("pv", "quad", (2, 4)),
             ("proj", "proj", (4, 6)), ("v", "v", (0, 0)), ("qk", "qk", (0, 0)),
             ("xt", "xt", (0, 0)), ("scores", "quad", (0, 0))))
        ACT_ORDER = (
            (("probs", "quad", (2, 3)), ("v", "v_out", (0, 0)), ("qk", "qk_out", (0, 0)),
             ("exp", "quad", (0, 1)), ("out", "quad", (2, 4)), ("outs", "outs", (0, 5)),
             ("v", "v_last", (0, 0)), ("qk", "qk_last", (0, 0)), ("xt", "xt", (0, 0))),
            (("probs", "quad", (2, 3)), ("v", "v_out", (0, 0)), ("qk", "qk_out", (0, 0)),
             ("exp", "quad", (0, 1)), ("out", "quad", (2, 4)),
             ("outs", "outs", (0, 5)), ("xt", "xt", (0, 0))))
        DVE_ORDER = (
            (("inverse", "quad", (1, 2)), ("out", "quad", (3, 5)),
             ("probs", "quad", (2, 3)), ("max", "quad", (0, 1)), ("residual", "residual", (4, 6)),
             ("v", "v_out", (0, 0)), ("qk", "qk_out", (0, 0)), ("outs", "outs", (0, 5)),
             ("stats", "stats", (0, 0)), ("aggr", "aggr", (0, 0)), ("norm", "norm", (0, 0)),
             ("v", "v_last", (0, 0)), ("qk", "qk_last", (0, 0)), ("xt", "xt", (0, 0))),
            (("inverse", "quad", (1, 2)), ("out", "quad", (3, 5)), ("max", "quad", (0, 1)),
             ("probs", "quad", (2, 3)), ("residual", "residual", (4, 6)), ("v", "v_out", (0, 0)),
             ("qk", "qk_out", (0, 0)), ("outs", "outs", (0, 5)), ("stats", "stats", (0, 0)),
             ("aggr", "aggr", (0, 0)), ("norm", "norm", (0, 0)), ("xt", "xt", (0, 0))))
        POOL_ORDER = ((("normalise", "quad", (1, 2)), ("bias", "bias", (4, 6)),
                       ("aggr", "aggr", (0, 0)), ("ctx", "ctx", (0, 0))),) * 2


        block = ctx.enter_context(nc.Block())

        @block.sync
        def _(sp):
            def tokens(g):
                sp.dma_start(xs[:, TILES * g:TILES * (g + 1), :], x[g]).then_inc(x_in[g > 0], 16)

            tokens(0)
            for i in range(4):
                sp.dma_start(wst[:, i, :], pieces[w_piece(i)]).then_inc(w_in[i], 16)
            sp.dma_start(b2raw, rows[0:1, 2 * D + 2 * EXPERTS:].to_broadcast(
                [P, EXPERTS * D])).then_inc(b2_in, 16)
            for j in range(4, N1 + N2):
                sp.wait_ge(w_split, j - 3)
                sp.dma_start(wst[:, j % 4, :], pieces[w_piece(j)]).then_inc(w_in[j % 4], 16)
                if 6 <= j < 5 + GROUPS:
                    tokens(j - 5)

            def context(g):
                sp.dma_start(craw[:, :].rearrange("p (k t) -> p k t", k=KD),
                             ctxT[g]).then_inc(c_in, 16)

            def experts(g):
                for j in range(4):
                    if isinstance(g, int):
                        sp.wait_ge(w_split, N1 + N2 - 3 + j)
                    else:
                        sp.wait_ge(e_split, g * 4 + j - 3)
                    sp.dma_start(wst[:, j, :], pieces[N1 + N2 + g * 4 + j]).then_inc(w_in[j], 16)

            context(0)
            with sp.Fori(1, GROUPS) as g:
                sp.wait_ge(c_lo, nth(CTX, 1, g, -1))
                context(g)
            experts(0)
            with sp.Fori(1, MCH // 4) as g:
                experts(g)
            with sp.Fori(0, GROUPS) as g:
                sp.wait_ge(fin, g + 1)
                sp.dma_start(out[g], yo).then_inc(out_dma, 16)
            sp.wait_ge(out_dma, GROUPS * 16)

        @block.tensor
        def _(pe):
            def three(acc, lhs, rhs, first=True, last=True, shared=False):
                for i, (a, b) in enumerate(((0, 0), (0, 1), (1, 0))):
                    mm = pe.matmul(acc, lhs[a], rhs[b], start=first and i == 0,
                                   stop=last and i == 2, skip_group_check=shared)
                return mm

            def project_qk(ph, g, job):
                c, is_k = job // 2, job % 2
                pe.wait_ge(qk_lo, nth(QK_F1, ph, g, job - 1))
                if job == 0:
                    pe.wait_ge(xt_lo, nth(GRP, ph, g, 0))
                if ph == 1 and job == 1:
                    pe.wait_ge(c_lo, nth(CTX, 1, g, 0))
                i = 4 * (c // 2) + is_k if ph == 0 else N1 + is_k
                col = (c % 2) * P
                pe.wait_ge(w_split, w_order(i))
                src = CT if ph == 1 and is_k else XT
                for k in range(KD):
                    mm = three(A0[:, :], [piece(i, s, k, col, col + P) for s in (0, 1)],
                               [src[:, s, k, :] for s in (0, 1)], k == 0, k == KD - 1)
                mm.then_inc(qk_ps, 1)

            def project_v(ph, g, job, part):
                if part != 1:
                    pe.wait_ge(v_lo, nth(VJ_F1, ph, g, job - 1))
                if ph == 0:
                    if job == 0:
                        pe.wait_ge(xt_lo, nth(GRP, ph, g, 0))
                    i, src, width, col = 4 * (job // 4) + 2, XT, 256, 0
                    tiles = [(job % 4, 0)]
                else:
                    if job == 0:
                        pe.wait_ge(c_lo, nth(CTX, 1, g, 0))
                    i, src, width, col = N1 + 2, CT, P, job * P
                    tiles = [(t, t * P) for t in (2 * part, 2 * part + 1)]
                pe.wait_ge(w_split, w_order(i))
                for t, to in tiles:
                    for k in range(KD):
                        mm = three(A1[:, to:to + width],
                                   [src[:, s, k, t * P:(t + 1) * P] for s in (0, 1)],
                                   [piece(i, s, k, col, col + width) for s in (0, 1)],
                                   k == 0, k == KD - 1)
                if part:
                    mm.then_inc(v_ps, 1)

            def scores(ph, g, n):
                c = n // 2
                if ph == 0:
                    r, rows = c % 2, slice(0, P)
                    if n % 2 == 0:
                        pe.wait_ge(qk_lo, nth(QK_F1, ph, g, 2 * c + 1))
                else:
                    r, rows = c // 4, slice(32 * (c % 4), 32 * (c % 4) + 32)
                    if n % 8 == 0:
                        pe.wait_ge(qk_lo, nth(QK_F1, ph, g, 2 * r + 1))
                pe.wait_ge(exped, nth(SLOT_F2, ph, g, n - 2))
                if ph == 1:
                    pe.sem_inc(pe_gate, 1)
                for j in range(2):
                    b = 2 * (n % 2) + j
                    mm = three(S[n % 2][:, 256 * j:256 * (j + 1)],
                               [Q[rows, r, s, b * P:(b + 1) * P] for s in (0, 1)],
                               [K[rows, r, s, b, :, :].rearrange("p h c -> p (h c)") for s in (0, 1)])
                mm.then_inc(scores_ps, 1)

            def transpose_probs(ph, g, n):
                pe.wait_ge(normed, nth(SLOT, ph, g, n))
                pe.wait_ge(pt_lo, nth(SLOT_F1, ph, g, n - 1))
                for u in range(4):
                    mm = pe.transpose(T[:, u * P:(u + 1) * P], probs[:, n % 4, u * P:(u + 1) * P],
                                      ident[:, :])
                mm.then_inc(pt_ps, 1)

            def probs_v(ph, g, n):
                c = n // 2
                pe.wait_ge(pt_lo, nth(SLOT_F1, ph, g, n))
                pe.wait_ge(o_lo, nth(SLOT_F1, ph, g, n - 1))
                if ph == 0:
                    cp = c // 2
                    if n % 4 < 2:
                        pe.wait_ge(v_lo, nth(VJ_F1, ph, g, 4 * cp + 2 * (n % 2) + 1))
                    for u in range(4):
                        b, h = 2 * (n % 2) + u // 2, u % 2
                        col = (c % 2) * P + h * DH1
                        mm = three(O[0:DH1, u * P:(u + 1) * P],
                                   [V[:, cp % 2, s, b, col:col + DH1] for s in (0, 1)],
                                   [PT[:, n % 2, s, u * P:(u + 1) * P] for s in (0, 1)])
                else:
                    if n % 8 == 0:
                        pe.wait_ge(v_lo, nth(VJ_F1, ph, g, n // 8))
                    for j in range(2):
                        b = 2 * (n % 2) + j
                        mm = three(O[0:32, j * 256:(j + 1) * 256],
                                   [V[:, 0, s, :, :].rearrange("p t c -> p (t c)")[:, (c // 4) * 512 + b * P + 32 * (c % 4):
                                                                        (c // 4) * 512 + b * P + 32 * (c % 4) + 32]
                                    for s in (0, 1)],
                                   [PT[:, n % 2, s, j * 256:(j + 1) * 256] for s in (0, 1)])
                mm.then_inc(pv_ps, 1)

            def project_out(ph, g, c, tiles):
                chunks = CHUNKS1 if ph == 0 else 2
                if ph == 0:
                    pe.wait_ge(o_lo, nth(SLOT_F1, ph, g, 2 * c + tiles[0] // 2))
                    i, k = 4 * (c // 2) + 3, c % 2
                else:
                    pe.wait_ge(at_lo, nth(ATC_F2, ph, g, c))
                    i, k = N1 + 3, c
                if c == 0:
                    pe.wait_ge(y_read, nth(GRP_F1, ph, g, -1))
                pe.wait_ge(w_split, w_order(i))
                for t in tiles:
                    mm = three(Y[t // 2][:, (t % 2) * D:(t % 2 + 1) * D],
                               [AT[:, c % 2, s, t * P:(t + 1) * P] for s in (0, 1)],
                               [piece(i, s, k, 0, D) for s in (0, 1)],
                               c == 0 and t % 2 == 0, c == chunks - 1, True)
                if tiles[-1] == TILES - 1:
                    mm.then_inc(oproj, 1)

            def transpose_tokens(ph, g, banks):
                pe.wait_ge(ln_x, nth(GRP, ph, g, 0))
                for k in range(KD):
                    for t in range(TILES):
                        mm = pe.transpose(banks[k][:, t * P:(t + 1) * P], xn[:, t, k * P:(k + 1) * P],
                                          ident[:, :])
                mm.then_inc(xt_ps, 1)

            def transpose_group(ph, g):
                if not (ph == 0 and isinstance(g, int) and g == 0):
                    pe.wait_ge(qk_lo, nth(QK_F1, ph, g, -1))
                    pe.wait_ge(v_lo, nth(VJ_F1, ph, g, -1))
                transpose_tokens(ph, g, A)

            pe.wait_ge(ready, 2)
            attentions(pe, PE_ORDER, {
                "scores": scores, "transpose": transpose_probs, "pv": probs_v, "proj": project_out,
                "qk": project_qk, "v": project_v, "xt": transpose_group})

            def up(g, m):
                pe.wait_ge(act_done, nth(MSTEP_F4, 2, g, m - 4))
                if m == 0:
                    pe.wait_ge(xt_lo, nth(GRP, 2, g, 0))
                pe.wait_ge(e_split, m + 1)
                for k in range(KD):
                    mm = three(H[m % 4][:, :], [arena[:, m * 2 * PIECE + s * PIECE + k * P:
                                                      m * 2 * PIECE + s * PIECE + (k + 1) * P]
                                                for s in (0, 1)],
                               [XT[:, s, k, :] for s in (0, 1)], k == 0, k == KD - 1)
                mm.then_inc(f1_ps, 1)

            def down(g, m):
                pe.wait_ge(h_lo, nth(MSTEP_F4, 2, g, m))
                if m == 0:
                    pe.wait_ge(y_read, nth(GRP_F1, 2, g, -1))
                for t in range(TILES):
                    mm = three(Y[t // 2][:, (t % 2) * D:(t % 2 + 1) * D],
                               [PT[:, m % 2, s, t * P:(t + 1) * P] for s in (0, 1)],
                               [piece(m, s, 1, 0, D) for s in (0, 1)],
                               m == 0 and t % 2 == 0, m == MCH - 1, True)
                mm.then_inc(f2_ps, 1)

            def logits(g):
                pe.wait_ge(xt_lo, nth(GRP, 2, g, 0))
                for t in range(TILES):
                    for i, (k, s) in enumerate(((0, 0), (0, 1), (1, 0), (1, 1))):
                        mm = pe.matmul(T[:, t * 2 * EXPERTS:(t + 1) * 2 * EXPERTS],
                                       XT[:, s, k, t * P:(t + 1) * P],
                                       gate[:, k, :, :].rearrange("p s e -> p (s e)"),
                                       start=i == 0, stop=i == 3)
                mm.then_inc(lg_ps, 1)

            def experts(g):
                last = isinstance(g, int) and g == GROUPS - 1
                for m in range(MCH + 2):
                    if m == MCH - 1 and not last:
                        pe.wait_ge(lg_v, g * LGV + 1)
                        transpose_tokens(2, g + 1, (T, O))
                    if m < MCH:
                        up(g, m)
                    if m == 1:
                        logits(g)
                    if m >= 2:
                        down(g, m - 2)

            with pe.Fori(0, GROUPS - 1) as g:
                experts(g)
            experts(GROUPS - 1)

        @block.scalar
        def _(act):
            act.dma_start(bias[:, :], biases).then_inc(b_in, 16)
            act.dma_start(rowc[:, :], rows[0:1, 0:2 * D + 2 * EXPERTS].to_broadcast(
                [P, 2 * D + 2 * EXPERTS])).then_inc(b_in, 16)
            act.dma_start(msk[:, :], mask).then_inc(b_in, 16)
            act.dma_start(gst[:, :], gateT).then_inc(b_in, 16)

            def tokens_hi(ph, g, banks):
                act.wait_ge(xt_ps, nth(GRP, ph, g, 0))
                for k in range(KD):
                    last = act.activation(XT[:, 0, k, :], banks[k][:, :], ACT.Copy)
                last.then_inc(xt_hi, 1)

            def weight_hi(i):
                j = w_order(i) - 1
                act.wait_ge(w_in[j % 4], 16 * (j // 4 + 1))
                scale = (DH1 ** -0.5 if i < N1 and i % 4 == 0 else DH2 ** -0.5 if i == N1 else 1.0)
                act.activation(arena[:, i * 2 * PIECE:i * 2 * PIECE + PIECE], wst[:, j % 4, :], ACT.Copy,
                               scale=scale).then_inc(w_hi, 1)

            def qk_evac(ph, g, job):
                c, is_k = job // 2, job % 2
                if ph == 0 and isinstance(g, int) and g == 0 and job == 0:
                    act.wait_ge(ready_v, 2)
                    act.wait_ge(ready, 3)
                act.wait_ge(qk_ps, nth(QK, ph, g, job))
                if not is_k:
                    col = (BQ1 if ph == 0 else BQ2) + c
                    last = act.activation(Q[:, c % 2, 0, :], A0[:, :], ACT.Identity,
                                          bias=bias[:, col:col + 1])
                elif ph == 0:
                    for h in range(2):
                        rows_ = slice(h * DH1, (h + 1) * DH1)
                        last = act.activation(K[rows_, c % 2, 0, :, h, :],
                                              A0[rows_, :].rearrange("p (b c) -> p b c", b=TILES),
                                              ACT.Identity, bias=bias[rows_, BK1 + c:BK1 + c + 1])
                else:
                    for h in range(2):
                        last = act.activation(K[:, c % 2, 0, :, h, :],
                                              A0[:, :].rearrange("p (b c) -> p b c", b=TILES),
                                              ACT.Identity, scale=half[:, h:h + 1],
                                              bias=bkh[:, 2 * c + h:2 * c + h + 1])
                last.then_inc(qk_hi, 1)

            def v_evac(ph, g, job):
                act.wait_ge(v_ps, nth(VJ, ph, g, job))
                if ph == 0:
                    cp, t = job // 4, job % 4
                    if t == 0 and (cp > 1 or not (isinstance(g, int) and g == 0)):
                        act.wait_ge(pv_ps, nth(SLOT_F2, ph, g, 4 * (cp - 1) - 1))
                    act.activation(V[:, cp % 2, 0, t, :], A1[:, 0:256], ACT.Copy).then_inc(v_hi, 1)
                else:
                    act.wait_ge(pv_ps, nth(SLOT_F2, ph, g, -5 if isinstance(g, int) else 8 * (job - 1) - 1))
                    act.activation(v2(0, job), A1[:, :], ACT.Copy).then_inc(v_hi, 1)

            def xt_evac(ph, g):
                tokens_hi(ph, g, A)


            def exp_probs(ph, g, n):
                act.wait_ge(maxed, nth(SLOT, ph, g, n))
                if (ph, n) == (0, 0) and isinstance(g, int):
                    act.wait_ge(b2_sum, 3)
                act.wait_ge(pt_ps, nth(SLOT_F4, ph, g, n - 4))
                for u in range(4):
                    last = act.activation(probs[:, n % 4, u * P:(u + 1) * P],
                                          S[n % 2][:, u * P:(u + 1) * P], ACT.Exp,
                                          bias=nm[:, n % 4, u:u + 1], accum_out=rsum[:, n % 4, u:u + 1])
                last.then_inc(exped, 1)

            def probs_hi(ph, g, n):
                act.wait_ge(pt_ps, nth(SLOT_F4, ph, g, n))
                act.wait_ge(pv_ps, nth(SLOT_F2, ph, g, n - 2))
                act.activation(PT[:, n % 2, 0, :], T[:, :], ACT.Copy).then_inc(pt_hi, 1)

            def out_hi(ph, g, n):
                c = n // 2
                act.wait_ge(pv_ps, nth(SLOT_F2, ph, g, n))
                if ph == 0:
                    if n % 2 == 0:
                        act.wait_ge(oproj, nth(OPROJ, ph, g, c - 2))
                    for h in range(2):
                        last = act.activation(
                            AT[h * DH1:(h + 1) * DH1, c % 2, 0, (n % 2) * 256:(n % 2 + 1) * 256]
                            .rearrange("p (b c) -> p b c", b=2),
                            O[0:DH1, :].rearrange("p (b h c) -> p b h c", b=2, h=2)[:, :, h, :],
                            ACT.Identity, bias=bias[0:DH1, BV1 + 2 * c + h:BV1 + 2 * c + h + 1])
                else:
                    if n % 8 == 0:
                        act.wait_ge(at_lo, nth(ATC_F2, ph, g, c // 4 - 2))
                    rows_ = slice(32 * (c % 4), 32 * (c % 4) + 32)
                    last = act.activation(
                        araw[rows_, c // 4, (n % 2) * 256:(n % 2 + 1) * 256]
                        .rearrange("p (b c) -> p b c", b=2),
                        O[0:32, :].rearrange("p (b h c) -> p b h c", b=2, h=2)[:, :, 0, :],
                        ACT.Copy, scale=half[0:32, 0:1])
                last.then_inc(o_hi, 1)

            def outs_hi(ph, g, cc):
                act.wait_ge(o_lo, nth(SLOT_F1, ph, g, 8 * cc + 7))
                act.wait_ge(oproj, nth(OPROJ, ph, g, cc - 2))
                act.activation(AT[:, cc, 0, :], araw[:, cc, :], ACT.Identity,
                               bias=bias[:, BV2 + cc:BV2 + cc + 1]).then_inc(at_hi, 1)

            def expert_hi(m):
                at = m * 2 * PIECE
                act.wait_ge(w_in[m % 4], 16 * ((N1 + N2 + m) // 4 + 1))
                act.activation(arena[:, at:at + PIECE], wst[:, m % 4, :], ACT.Copy).then_inc(e_hi, 1)

            def weights(ph, g, n):
                if ph == 2 and DRAIN - LEAD <= n < DRAIN:
                    expert_hi(n - DRAIN + LEAD)
                if ph == 0 and isinstance(g, int):
                    for i in weight_slots(n):
                        weight_hi(i)
                    if n == 15:
                        act.activation(gate[:, :, 0, :], gst[:, :].rearrange("p (k e) -> p k e", k=KD),
                                       ACT.Copy).then_inc(w_hi, 1)

            attentions(act, ACT_ORDER, {
                "exp": exp_probs, "probs": probs_hi, "out": out_hi, "qk": qk_evac, "v": v_evac,
                "outs": outs_hi, "xt": xt_evac, "slot": weights})

            def experts(g):
                last = isinstance(g, int) and g == GROUPS - 1
                for m in range(MCH):
                    act.wait_ge(f1_ps, nth(MSTEP, 2, g, m))
                    act.wait_ge(h_lo, nth(MSTEP_F4, 2, g, m - 4))
                    act.activation(probs[:, m % 4, :], H[m % 4][:, :], ACT.Gelu,
                                   bias=bias[:, B1 + m:B1 + m + 1]).then_inc(act_done, 1)
                    act.wait_ge(act_done, nth(MSTEP_F4, 2, g, m))
                    act.wait_ge(f2_ps, nth(MSTEP_F2, 2, g, m - 2))
                    act.activation(PT[:, m % 2, 0, :], probs[:, m % 4, :], ACT.Copy).then_inc(h_hi, 1)
                    if isinstance(g, int) and g == 0 and m + LEAD < MCH:
                        expert_hi(m + LEAD)
                    if m == 12:
                        act.wait_ge(lg_v, g * LGV + 8)
                        act.activation(lg[:, 4, :], lg[:, 3, :], ACT.Exp, scale=2.0).then_inc(lg_exp, 1)
                if not last:
                    tokens_hi(2, g + 1, (T, O))

            experts(0)
            with act.Fori(1, GROUPS - 1) as g:
                experts(g)
            experts(GROUPS - 1)


        @block.vector
        def _(dve):
            def sub_lo(out_, src, hi, sem_):
                dve.tensor_tensor(out_, src, hi.bitcast(F32), ALU.subtract).then_inc(sem_, 1)

            def ln_stats(ph, g, t):
                tile_ = (g * TILES + t)
                dve.bn_stats(st[:, t, :], xs[:, tile_, :] if isinstance(tile_, int) else
                             xs[:, bass.ds(tile_, 1), :].rearrange("p a d -> p (a d)")
                             ).then_inc(ln_stat, 1)

            def ln_finish(ph, g):
                dve.wait_ge(ln_stat, nth(LNST, ph, g, TILES - 1))
                dve.sem_inc(dve_gate, 1)
                for t in range(TILES):
                    last = dve.bn_aggr(mv[:, t, :], st[:, t, :])
                last.then_inc(ln_aggr, 1)
                dve.wait_ge(ln_aggr, nth(GRP, ph, g, 0))
                dve.tensor_scalar(ve[:, :], mv[:, :, 1], LN_EPS, None, ALU.add).then_inc(ln_var, 1)

            def ln_apply(ph, g):
                dve.wait_ge(ln_rstd, nth(GRP, ph, g, 0))
                if not (ph == 0 and isinstance(g, int) and g == 0):
                    dve.wait_ge(xt_ps, nth(GRP, ph, g, -1))
                for t in range(TILES):
                    tile_ = g * TILES + t
                    src = xs[:, tile_, :] if isinstance(tile_, int) else \
                        xs[:, bass.ds(tile_, 1), :].rearrange("p a d -> p (a d)")
                    last = dve.tensor_scalar(xn[:, t, :], src, mv[:, t, 0:1], rstd[:, t:t + 1],
                                             ALU.subtract, ALU.mult)
                last.then_inc(ln_x, 1)

            def tokens_lo(ph, g, banks):
                dve.wait_ge(xt_hi, nth(GRP, ph, g, 0))
                for k in range(KD):
                    last = dve.tensor_tensor(XT[:, 1, k, :], banks[k][:, :], XT[:, 0, k, :].bitcast(F32),
                                             ALU.subtract)
                last.then_inc(xt_lo, 1)

            def weight_lo(i):
                dve.wait_ge(w_hi, w_order(i))
                scale = (DH1 ** -0.5 if i < N1 and i % 4 == 0 else DH2 ** -0.5 if i == N1 else 1.0)
                at = i * 2 * PIECE
                dve.scalar_tensor_tensor(arena[:, at + PIECE:at + 2 * PIECE], wst[:, (w_order(i) - 1) % 4, :], scale,
                                         arena[:, at:at + PIECE].bitcast(F32), ALU.mult,
                                         ALU.subtract).then_inc(w_split, 1)

            def qk_low(ph, g, job):
                c, is_k = job // 2, job % 2
                dve.wait_ge(qk_hi, nth(QK, ph, g, job))
                if not is_k:
                    col = (BQ1 if ph == 0 else BQ2) + c
                    last = dve.scalar_tensor_tensor(Q[:, c % 2, 1, :], A0[:, :], bias[:, col:col + 1],
                                                    Q[:, c % 2, 0, :].bitcast(F32), ALU.add, ALU.subtract)
                elif ph == 0:
                    for h in range(2):
                        rows_ = slice(h * DH1, (h + 1) * DH1)
                        last = dve.scalar_tensor_tensor(
                            K[rows_, c % 2, 1, :, h, :],
                            A0[rows_, :].rearrange("p (b c) -> p b c", b=TILES),
                            bias[rows_, BK1 + c:BK1 + c + 1],
                            K[rows_, c % 2, 0, :, h, :].bitcast(F32), ALU.add, ALU.subtract)
                else:
                    dve.tensor_scalar(A0[:, :], A0[:, :], bias[:, BK2 + c:BK2 + c + 1], None,
                                      ALU.add).then_inc(kbias, 1)
                    dve.wait_ge(kbias, nth(ATC, 1, g, c))
                    for h in range(2):
                        last = dve.scalar_tensor_tensor(
                            K[:, c % 2, 1, :, h, :], A0[:, :].rearrange("p (b c) -> p b c", b=TILES),
                            half[:, h:h + 1], K[:, c % 2, 0, :, h, :].bitcast(F32),
                            ALU.mult, ALU.subtract)
                last.then_inc(qk_lo, 1)

            def v_low(ph, g, job):
                dve.wait_ge(v_hi, nth(VJ, ph, g, job))
                if ph == 0:
                    r, t = job // 4 % 2, job % 4
                    sub_lo(V[:, r, 1, t, :], A1[:, 0:256], V[:, r, 0, t, :], v_lo)
                else:
                    sub_lo(v2(1, job), A1[:, :], v2(0, job), v_lo)

            def constants():
                dve.wait_ge(b_in, 64)
                dve.wait_ge(ready, 2)
                for h in range(2):
                    dve.tensor_reduce(half[:, h:h + 1],
                                      ident[:, :].rearrange("p (a h c) -> p a h c", a=4, h=2)[:, :, h, :],
                                      axis=AX.XY, op=ALU.add).then_inc(half_built, 1)
                dve.tensor_scalar(bias[:, BQ1:BQ1 + 8], bias[:, BQ1:BQ1 + 8], DH1 ** -0.5, None, ALU.mult)
                dve.tensor_scalar(bias[:, BQ2:BQ2 + 2], bias[:, BQ2:BQ2 + 2], DH2 ** -0.5, None, ALU.mult)
                dve.tensor_scalar(dropped[:, :], msk[:, :], 0.0, None, ALU.is_equal)
                dve.memset(neg[:, :], MASKED)
                dve.wait_ge(half_built, 2)
                for c in range(2):
                    for h in range(2):
                        last = dve.tensor_tensor(bkh[:, 2 * c + h:2 * c + h + 1], bias[:, BK2 + c:BK2 + c + 1],
                                                 half[:, h:h + 1], ALU.mult)
                last.then_inc(ready_v, 1)

            dve.memset(mhalf[:, :], -0.5).then_inc(ready_v, 1)

            def row_max(ph, g, n):
                dve.wait_ge(scores_ps, nth(SLOT, ph, g, n))
                s3 = S[n % 2][:, :].rearrange("p (u c) -> p u c", u=4)
                if ph == 1:
                    dve.sem_inc(dve_gate, 1)
                    dve.copy_predicated(s3, dropped[:, :].unsqueeze(1).to_broadcast([P, 4, P]),
                                        neg[:, :].unsqueeze(2).to_broadcast([P, 4, P])
                                        ).then_inc(filled, 1)
                    dve.wait_ge(filled, g * QUADS + n + 1)
                dve.tensor_reduce(nm[:, n % 4, :], s3, axis=AX.X, op=ALU.max, negate=True
                                  ).then_inc(maxed, 1)

            def row_inverse(ph, g, n):
                dve.wait_ge(exped, nth(SLOT_F2, ph, g, n))
                dve.reciprocal(rinv[:, n % 4, :], rsum[:, n % 4, :]).then_inc(inverted, 1)

            def probs_low(ph, g, n):
                dve.wait_ge(pt_hi, nth(SLOT, ph, g, n))
                sub_lo(PT[:, n % 2, 1, :], T[:, :], PT[:, n % 2, 0, :], pt_lo)

            def out_low(ph, g, n):
                c = n // 2
                dve.wait_ge(o_hi, nth(SLOT, ph, g, n))
                o4 = O[:, :].rearrange("p (b h c) -> p b h c", b=2, h=2)
                cols = slice((n % 2) * 256, (n % 2 + 1) * 256)
                if ph == 0:
                    for h in range(2):
                        rows_ = slice(h * DH1, (h + 1) * DH1)
                        last = dve.scalar_tensor_tensor(
                            AT[rows_, c % 2, 1, cols].rearrange("p (b c) -> p b c", b=2),
                            o4[0:DH1, :, h, :], bias[0:DH1, BV1 + 2 * c + h:BV1 + 2 * c + h + 1],
                            AT[rows_, c % 2, 0, cols].rearrange("p (b c) -> p b c", b=2).bitcast(F32),
                            ALU.add, ALU.subtract)
                else:
                    rows_ = slice(32 * (c % 4), 32 * (c % 4) + 32)
                    dst = araw[rows_, c // 4, cols].rearrange("p (b c) -> p b c", b=2)
                    last = dve.scalar_tensor_tensor(dst, o4[0:32, :, 1, :], half[0:32, 1:2], dst,
                                                    ALU.mult, ALU.add)
                last.then_inc(o_lo, 1)

            def add_residual(ph, g):
                dve.wait_ge(oproj, nth(OPROJ, ph, g, OPROJ.per[ph] - 1))
                for j in range(2):
                    at = g * TILES + 2 * j
                    dst = xs[:, bass.ds(at, 2), :] if not isinstance(at, int) else xs[:, at:at + 2, :]
                    last = dve.tensor_tensor(dst, Y[j][:, :].rearrange("p (t d) -> p t d", t=2), dst,
                                             ALU.add)
                last.then_inc(y_read, 1)

            def outs_low(ph, g, cc):
                dve.wait_ge(at_hi, nth(ATC, ph, g, cc))
                dve.scalar_tensor_tensor(AT[:, cc, 1, :], araw[:, cc, :], bias[:, BV2 + cc:BV2 + cc + 1],
                                         AT[:, cc, 0, :].bitcast(F32), ALU.add,
                                         ALU.subtract).then_inc(at_lo, 1)

            def stats(ph, g):
                if ph == 0:
                    dve.wait_ge(x_in[not (isinstance(g, int) and g == 0)],
                                16 if isinstance(g, int) and g == 0 else (GROUPS - 1) * 16)
                else:
                    dve.wait_ge(x_ready, nth(GRP, ph - 1, g, 0))
                    dve.sem_inc(dve_gate, 1)
                for t in range(TILES):
                    ln_stats(ph, g, t)

            def xt_low(ph, g):
                tokens_lo(ph, g, A)

            def expert_lo(m):
                at = m * 2 * PIECE
                dve.wait_ge(e_hi, m + 1)
                sub_lo(arena[:, at + PIECE:at + 2 * PIECE], wst[:, m % 4, :], arena[:, at:at + PIECE],
                       e_split)

            def weights(ph, g, n):
                if ph == 2 and DRAIN - LEAD <= n < DRAIN:
                    expert_lo(n - DRAIN + LEAD)
                if ph == 0 and isinstance(g, int):
                    for i in weight_slots(n):
                        weight_lo(i)
                    if g == 0 and n == XT_AT:
                        constants()
                    if n == 15:
                        dve.wait_ge(w_hi, N1 + N2 + 1)
                        sub_lo(gate[:, :, 1, :], gst[:, :].rearrange("p (k e) -> p k e", k=KD),
                               gate[:, :, 0, :], w_split)

            attentions(dve, DVE_ORDER, {
                "max": row_max, "inverse": row_inverse, "probs": probs_low, "out": out_low,
                "qk": qk_low, "v": v_low, "outs": outs_low, "residual": add_residual, "stats": stats,
                "aggr": ln_finish, "norm": ln_apply, "xt": xt_low, "slot": weights})

            def gating(g, step):
                def after(n):
                    dve.wait_ge(lg_v, g * LGV + n)

                def l3(i):
                    return lg[:, i, :].rearrange("p (t e) -> p t e", t=TILES)

                def row(i):
                    return rowc[:, 2 * D + i * EXPERTS:2 * D + (i + 1) * EXPERTS].unsqueeze(1) \
                        .to_broadcast([P, TILES, EXPERTS])

                def col(i):
                    return gs[:, i, :].unsqueeze(2).to_broadcast([P, TILES, EXPERTS])

                if step == 0:
                    dve.wait_ge(lg_ps, g + 1)
                    t4 = T[:, 0:TILES * 2 * EXPERTS].rearrange("p (t s e) -> p t s e", t=TILES, s=2)
                    dve.tensor_tensor(l3(4), t4[:, :, 0, :], row(0), ALU.add).then_inc(lg_a, 1)
                    dve.wait_ge(lg_a, g + 1)
                    dve.tensor_tensor(l3(0), t4[:, :, 1, :], l3(4), ALU.add).then_inc(lg_v, 1)
                elif step == 1:
                    after(1)
                    dve.tensor_tensor(lg[:, 1, :], lg[:, 0, :], lg[:, 0, :], ALU.mult).then_inc(lg_v, 1)
                elif step == 2:
                    after(2)
                    dve.tensor_reduce(gs[:, 0, :], l3(1), axis=AX.X, op=ALU.add).then_inc(lg_v, 1)
                elif step == 3:
                    after(3)
                    dve.tensor_scalar(gs[:, 1, :], gs[:, 0, :], 1.0 / EXPERTS, F32_EPS, ALU.mult,
                                      ALU.add).then_inc(lg_v, 1)
                elif step == 4:
                    dve.wait_ge(lg_pow, g + 1)
                    dve.tensor_tensor(l3(1), l3(0), col(2), ALU.mult).then_inc(lg_v, 1)
                elif step == 5:
                    after(5)
                    dve.tensor_tensor(l3(2), l3(1), row(1), ALU.mult).then_inc(lg_v, 1)
                elif step == 6:
                    after(6)
                    dve.tensor_reduce(gs[:, 3, :], l3(2), axis=AX.X, op=ALU.max).then_inc(lg_v, 1)
                elif step == 7:
                    after(7)
                    dve.tensor_tensor(l3(3), l3(2), col(3), ALU.subtract).then_inc(lg_v, 1)
                elif step == 8:
                    dve.wait_ge(lg_exp, g + 1)
                    dve.tensor_reduce(gs[:, 4, :], l3(4), axis=AX.X, op=ALU.add).then_inc(lg_v, 1)
                elif step == 9:
                    after(9)
                    dve.reciprocal(gs[:, 5, :], gs[:, 4, :]).then_inc(lg_v, 1)
                elif step == 10:
                    after(10)
                    dve.tensor_scalar(gs[:, 6, :], gs[:, 5, :], 1e-6, None, ALU.add).then_inc(lg_v, 1)
                elif step == 11:
                    after(11)
                    dve.reciprocal(gs[:, 3, :], gs[:, 6, :]).then_inc(lg_v, 1)
                elif step == 12:
                    after(12)
                    dve.tensor_tensor(gs[:, 7, :], gs[:, 5, :], gs[:, 3, :], ALU.mult).then_inc(ng_done, 1)

            def finish(g):
                dve.wait_ge(f2_ps, nth(MSTEP_F2, 2, g, MCH - 1))
                if not (isinstance(g, int) and g == 0):
                    dve.wait_ge(out_dma, g * 16)
                for j in range(2):
                    last = dve.tensor_tensor(yo[:, 2 * j:2 * j + 2, :],
                                             Y[j][:, :].rearrange("p (t d) -> p t d", t=2),
                                             b2sum[:, :].unsqueeze(1).to_broadcast([P, 2, D]), ALU.add)
                last.then_inc(y_read, 1)
                dve.wait_ge(y_read, nth(GRP_F1, 2, g, 0))
                dve.wait_ge(ng_done, g + 1)
                for t in range(TILES):
                    at = g * TILES + t
                    src = xs[:, at, :] if isinstance(at, int) else \
                        xs[:, bass.ds(at, 1), :].rearrange("p a d -> p (a d)")
                    last = dve.scalar_tensor_tensor(yo[:, t, :], yo[:, t, :], gs[:, 7, t:t + 1], src,
                                                    ALU.mult, ALU.add)
                last.then_inc(fin, 1)

            def experts(g):
                last = isinstance(g, int) and g == GROUPS - 1
                for m in range(MCH):
                    dve.wait_ge(h_hi, nth(MSTEP, 2, g, m))
                    sub_lo(PT[:, m % 2, 1, :], probs[:, m % 4, :], PT[:, m % 2, 0, :], h_lo)
                    if isinstance(g, int) and g == 0 and m + LEAD < MCH:
                        expert_lo(m + LEAD)
                    if 4 <= m <= 11:
                        gating(g, m - 4)
                    if 14 <= m <= 18:
                        gating(g, m - 6)
                    if not last:
                        if 20 <= m < 24:
                            if m == 20:
                                dve.wait_ge(x_ready, nth(GRP, 1, g + 1, 0))
                                dve.sem_inc(dve_gate, 1)
                            ln_stats(2, g + 1, m - 20)
                        if m == 24:
                            ln_finish(2, g + 1)
                        if m == 28:
                            ln_apply(2, g + 1)
                if not last:
                    tokens_lo(2, g + 1, (T, O))
                finish(g)

            experts(0)
            with dve.Fori(1, GROUPS - 1) as g:
                experts(g)
            experts(GROUPS - 1)

        @block.gpsimd
        def _(pool):
            for s, c in ((pt_ps, 4), (exped, 2), (pv_ps, 2), (pt_lo, 1), (o_lo, 1), (oproj, 2),
                         (qk_lo, 1), (v_lo, 1), (y_read, 1), (act_done, 4), (h_lo, 4), (f2_ps, 2), (at_lo, 2)):
                pool.sem_inc(s, c)
            pool.memset(ident[:, :], 0.0).then_inc(ready, 1)
            pool.wait_ge(ready, 1)
            pool.affine_select(out=ident[:, :], in_=ident[:, :], compare_op=ALU.not_equal, fill=1.0,
                               base=0, pattern=[[-1, P]], channel_multiplier=1).then_inc(ready, 1)
            pool.memset(K.rearrange("p r s b h c -> p (r s b h c)").bitcast(F32), 0.0).then_inc(ready, 1)

            def inv_sqrt(ph, g):
                if ph == 0 and isinstance(g, int) and g == 0:
                    pool.wait_ge(ready_v, 1)
                pool.wait_ge(ln_var, nth(GRP, ph, g, 0))
                pool.tensor_tensor(rstd[:, :], ve[:, :], mhalf[:, :], ALU.pow).then_inc(ln_rstd, 1)

            def normalise(ph, g, n):
                pool.wait_ge(inverted, nth(SLOT, ph, g, n))
                p3 = probs[:, n % 4, :].rearrange("p (u c) -> p u c", u=4)
                pool.tensor_tensor(p3, p3, rinv[:, n % 4, :].unsqueeze(2).to_broadcast([P, 4, P]),
                                   ALU.mult).then_inc(normed, 1)

            def out_bias(ph, g, part):
                if part == 0:
                    pool.wait_ge(y_read, nth(GRP_F1, ph, g, 0))
                    pool.sem_inc(pool_gate, 1)
                at = g * TILES + 2 * part
                dst = xs[:, at:at + 2, :] if isinstance(at, int) else xs[:, bass.ds(at, 2), :]
                add = pool.tensor_tensor(dst, dst, rowc[:, ph * D:(ph + 1) * D].unsqueeze(1)
                                         .to_broadcast([P, 2, D]), ALU.add)
                if part == 1:
                    add.then_inc(x_ready, 1)

            def split_context(ph, g, part):
                k = part % 2
                raw, hi, lo = craw[:, k * GT:(k + 1) * GT], CT[:, 0, k, :], CT[:, 1, k, :]
                if part == 0:
                    pool.wait_ge(c_in, nth(CTX, 1, g, 0) * 16)
                    if not isinstance(g, int):
                        pool.wait_ge(qk_ps, nth(QK, 1, g, -1))
                        pool.wait_ge(v_ps, nth(VJ, 1, g, -1))
                    pool.sem_inc(pool_gate, 1)
                if part < 2:
                    rounded = pool.tensor_copy(hi, raw)
                    if part == 1:
                        rounded.then_inc(c_hi, 1)
                    return
                if part == 2:
                    pool.wait_ge(c_hi, nth(CTX, 1, g, 0))
                rest = pool.tensor_tensor(lo, raw, hi.bitcast(F32), ALU.subtract)
                if part == 3:
                    rest.then_inc(c_lo, 1)

            def sum_b2(ph, g, n):
                if (ph, n) == (0, 1) and isinstance(g, int):
                    pool.wait_ge(b2_in, 16)
                    for i, w in enumerate((EXPERTS * D // 2, EXPERTS * D // 4)):
                        pool.tensor_tensor(b2raw[:, 0:w], b2raw[:, 0:w], b2raw[:, w:2 * w],
                                           ALU.add).then_inc(b2_sum, 1)
                        pool.wait_ge(b2_sum, i + 1)
                    pool.tensor_tensor(b2sum[:, :], b2raw[:, 0:D], b2raw[:, D:2 * D],
                                       ALU.add).then_inc(b2_sum, 1)

            attentions(pool, POOL_ORDER, {
                "slot": sum_b2,
                "normalise": normalise, "bias": out_bias, "ctx": split_context, "aggr": inv_sqrt})

            def inv_rms(g):
                pool.wait_ge(lg_v, g * LGV + 4)
                pool.tensor_tensor(gs[:, 2, :], gs[:, 1, :], mhalf[:, :], ALU.pow).then_inc(lg_pow, 1)

            inv_rms(0)
            inv_sqrt(2, 1)
            with pool.Fori(1, GROUPS - 1) as g:
                inv_rms(g)
                inv_sqrt(2, g + 1)
            inv_rms(GROUPS - 1)


_OUT = (16, 128, 256)


def kernel(**inputs):
    import numpy as np
    import concourse.bacc as bacc
    from concourse.bass_utils import run_bass_kernel_spmd as run

    f = {k: np.asarray(v) for k, v in inputs.items()}

    def halves(w):
        n = w.shape[1] // 256
        return w.reshape(2, P, n, 256).transpose(2, 1, 0, 3).reshape(n, P, PIECE)

    wq, wk, wv = (halves(f["L0_attn_W_" + c].reshape(HEADS * DH1, D).T) for c in "QKV")
    wo = f["L0_attn_W_O"].transpose(0, 2, 1).reshape(4, 2, P, D).transpose(0, 2, 1, 3).reshape(4, P, PIECE)
    first = np.stack([wq, wk, wv, wo], axis=1).reshape(N1, P, PIECE)
    second = np.concatenate([halves(f["L0_xattn_W" + c].T) for c in "qkvo"])
    w1 = f["L0_ffn_w1"].transpose(1, 0, 2).reshape(KD, P, MCH, P).transpose(2, 1, 0, 3).reshape(MCH, P, 256)
    w2 = f["L0_ffn_w2"].reshape(MCH, P, D)
    pieces = np.concatenate([first, second, np.concatenate([w1, w2], axis=2)])

    bv1 = np.concatenate([f["L0_attn_b_V"].reshape(HEADS, DH1).T] * 2)
    biases = np.concatenate(
        [f["L0_attn_b_Q"].reshape(8, P).T, f["L0_attn_b_K"].reshape(8, P).T, bv1]
        + [f["L0_xattn_b" + c].reshape(2, P).T for c in "qkv"] + [f["L0_ffn_b1"].reshape(MCH, P).T], axis=1)
    rows = np.concatenate([f["L0_attn_b_O"], f["L0_xattn_bo"], f["L0_ffn_gate_b"], f["L0_ffn_rms_w"],
                           f["L0_ffn_b2"].reshape(-1)]).reshape(1, -1)
    gateT = f["L0_ffn_gate_w"].T.reshape(KD, P, EXPERTS).transpose(1, 0, 2).reshape(P, KD * EXPERTS)
    x = f["x"].reshape(GROUPS, TILES, P, D).transpose(0, 2, 1, 3)
    ctxT = f["ctx_1024"].reshape(GROUPS, GT, KD, P).transpose(0, 3, 2, 1)
    mask = f["mask_1x1xSxS2_bk0"].reshape(P, P)

    nc = bacc.Bacc("TRN2", target_bir_lowering=False, num_devices=1)
    arrays, args = {}, []
    for name, a in (("x", x), ("ctxT", ctxT), ("mask", mask), ("pieces", pieces), ("gateT", gateT),
                    ("biases", biases), ("rows", rows)):
        a = np.ascontiguousarray(a)
        arrays["in_" + name] = a
        args.append(nc.dram_tensor("in_" + name, a.shape, mybir.dt.from_np(a.dtype),
                                   kind="ExternalInput").ap())
    args.append(nc.dram_tensor("out_0", (GROUPS, P, TILES, D), F32, kind="ExternalOutput").ap())
    build(nc, *args)
    got = run(nc, [arrays], core_ids=[0]).results[0]["out_0"]
    return got.transpose(0, 2, 1, 3).reshape(_OUT)
```

```python
from collections import namedtuple
from contextlib import ExitStack

import concourse.bass as bass
from concourse import mybir

F32 = mybir.dt.float32
F32R = mybir.dt.float32r
U8 = mybir.dt.uint8
ALU = mybir.AluOpType
ACT = mybir.ActivationFunctionType
AX = mybir.AxisListType

P = 128
D = 256
KD = D // P
GROUPS = 4
TILES = 4
GT = TILES * P
QUADS = 16
PERIOD = QUADS
HEADS = 16
DH1, DH2 = 64, 16
CHUNKS1 = HEADS * DH1 // P
EXPERTS, HID = 8, 512
MCH = EXPERTS * HID // P
PIECE = 512
N1, N2 = 16, 4
LN_EPS = 1e-5
F32_EPS = 1.1920928955078125e-07
MASKED = -1e9

BQ1, BK1, BV1 = 0, 8, 16
BQ2, BV2, B1 = 32, 34, 42
NBIAS = B1 + MCH

Count = namedtuple("Count", "credit per")


def nth(count, ph, g, i):
    return count.credit + GROUPS * sum(count.per[:ph]) + g * count.per[ph] + i + 1


SLOT = Count(0, (16, 16, 0))
SLOT_F1 = Count(1, (16, 16, 0))
OUT = Count(0, (16, 8, 0))
OUT_F1 = Count(1, (16, 8, 0))
SLOT_F2 = Count(2, (16, 16, 0))
SLOT_F4 = Count(4, (16, 16, 0))
QK = Count(0, (16, 4, 0))
QK_F1 = Count(1, (16, 4, 0))
VJ = Count(0, (16, 2, 0))
VJ_F1 = Count(1, (16, 2, 0))
OPROJ = Count(2, (8, 2, 0))
GRP = Count(0, (1, 1, 1))
GRP_F1 = Count(1, (1, 1, 1))
CTX = Count(0, (0, 1, 0))
MSTEP = Count(0, (0, 0, MCH))
MSTEP_F2 = Count(2, (0, 0, MCH))
MSTEP_F4 = Count(4, (0, 0, MCH))
XTE = Count(0, (KD, KD, KD))
LNST = Count(0, (TILES, TILES, TILES))


def build(nc, x, ctxT, mask, pieces, gateT, biases, rows, out):
    with ExitStack() as ctx:
        def sb(name, shape, dt):
            return ctx.enter_context(nc.sbuf_tensor(name, shape, dt))

        def bank(name):
            return ctx.enter_context(nc.psum_tensor(name, [P, 512], F32))

        def sem(name):
            return ctx.enter_context(nc.semaphore(name))

        arena = sb("arena", [P, MCH * 2 * PIECE], F32R)
        work = (N1 + N2) * 2 * PIECE

        def piece(i, lo, k, a, b):
            at = i * 2 * PIECE + lo * PIECE + k * 256
            return arena[:, at + a:at + b]

        def region(cols):
            nonlocal work
            at = work
            work += cols
            return arena[:, at:at + cols]

        V = region(4096).rearrange("p (r s t c) -> p r s t c", r=2, s=2, t=TILES)
        K = region(4096).rearrange("p (r s b h c) -> p r s b h c", r=2, s=2, b=TILES, h=2)
        Q = region(2048).rearrange("p (r s c) -> p r s c", r=2, s=2)
        AT = region(2048).rearrange("p (r s c) -> p r s c", r=2, s=2)
        assert work == MCH * 2 * PIECE
        V2 = arena[:, 0:4096].rearrange("p (j s t c) -> p j s t c", s=2, j=2, t=TILES)

        PT = sb("PT", [P, 2, 2, 512], F32R)
        XT = sb("XT", [P, 2, KD, GT], F32R)
        CT = sb("CT", [P, 2, KD, GT], F32R)
        gate = sb("gate", [P, KD, 2, EXPERTS], F32R)
        probs = sb("probs", [P, 4, 512], F32)
        xs = sb("xs", [P, GROUPS * TILES, D], F32)
        xn = sb("xn", [P, TILES, D], F32)
        craw = sb("craw", [P, KD * GT], F32)
        yo = craw[:, :].rearrange("p (t d) -> p t d", t=TILES)
        wst = sb("wst", [P, 4, PIECE], F32)
        ident = sb("ident", [P, P], F32)
        bias = sb("bias", [P, NBIAS], F32)
        rowc = sb("rowc", [P, 2 * D + 2 * EXPERTS], F32)
        b2sum = sb("b2sum", [P, D], F32)
        gst = sb("gst", [P, KD * EXPERTS], F32)
        msk = sb("msk", [P, P], U8)
        dropped = sb("dropped", [P, P], U8)
        neg = sb("neg", [P, 1], F32)
        half = sb("half", [P, 2], F32)
        bkraw = sb("bkraw", [2, D], F32)
        bkhi = sb("bkhi", [2, D], F32R)
        bklo = sb("bklo", [2, D], F32)
        bkrow = sb("bkrow", [2, D], F32R)
        ones = sb("ones", [2, GT], F32R)
        mhalf = sb("mhalf", [P, TILES], F32)
        nm = sb("nm", [P, 4, 4], F32)
        rsum = sb("rsum", [P, 4, 4], F32)
        rinv = sb("rinv", [P, 4, 4], F32)
        st = sb("st", [P, TILES, 6], F32)
        mv = sb("mv", [P, TILES, 2], F32)
        ve = sb("ve", [P, TILES], F32)
        rstd = sb("rstd", [P, TILES], F32)
        lg = sb("lg", [P, 5, TILES * EXPERTS], F32)
        gs = sb("gs", [P, 8, TILES], F32)
        b2raw = probs[:, :, :].rearrange("p r c -> p (r c)")

        A0, A1, S0, S1, T, O, Y0, Y1 = (bank(n) for n in ("A0", "A1", "S0", "S1", "T", "O", "Y0", "Y1"))
        S, Y = (S0, S1), (Y0, Y1)
        H = (S0, S1, A0, A1)

        x_in = [sem("x_in0"), sem("x_in")]
        b_in = sem("b_in")
        b2_in = sem("b2_in")
        b2_sum = sem("b2_sum")
        c_in = sem("c_in")
        w_in = [sem(f"w_in{i}") for i in range(4)]
        out_dma = sem("out_dma")
        ready = sem("ready")
        ready_v = sem("ready_v")
        w_hi = sem("w_hi")
        w_split = sem("w_split")
        e_hi = sem("e_hi")
        e_split = sem("e_split")
        scores_ps = sem("scores_ps")
        filled = sem("filled")
        maxed = sem("maxed")
        exped = sem("exped")
        inverted = sem("inverted")
        normed = sem("normed")
        pt_ps = sem("pt_ps")
        pt_hi = sem("pt_hi")
        pt_lo = sem("pt_lo")
        pv_ps = sem("pv_ps")
        o_hi = sem("o_hi")
        o_lo = sem("o_lo")
        v_zero = sem("v_zero")
        oproj = sem("oproj")
        qk_ps = sem("qk_ps")
        qk_hi = sem("qk_hi")
        qk_lo = sem("qk_lo")
        v_ps = sem("v_ps")
        v_hi = sem("v_hi")
        v_lo = sem("v_lo")
        xt_ps = sem("xt_ps")
        xt_hi = sem("xt_hi")
        xt_lo = sem("xt_lo")
        c_hi = sem("c_hi")
        c_lo = sem("c_lo")
        y_read = sem("y_read")
        x_ready = sem("x_ready")
        ln_stat = sem("ln_stat")
        ln_aggr = sem("ln_aggr")
        ln_var = sem("ln_var")
        ln_rstd = sem("ln_rstd")
        ln_x = sem("ln_x")
        f1_ps = sem("f1_ps")
        act_done = sem("act_done")
        h_hi = sem("h_hi")
        h_lo = sem("h_lo")
        f2_ps = sem("f2_ps")
        lg_ps = sem("lg_ps")
        lg_v = sem("lg_v")
        lg_a = sem("lg_a")
        lg_pow = sem("lg_pow")
        lg_exp = sem("lg_exp")
        fin = sem("fin")
        half_built = sem("half_built")
        ng_done = sem("ng_done")
        pe_gate = sem("pe_gate")
        dve_gate = sem("dve_gate")
        pool_gate = sem("pool_gate")
        LGV = 12

        XT_AT = 3
        SCORES = XT_AT + 4

        def steps(name, ph, v, lag=0):
            v -= lag
            if name == "quad":
                q = v - SCORES
                return [(q,)] if 0 <= q < QUADS else []
            if name == "qk":
                jobs = {XT_AT + 1 + j: j for j in range(16)} if ph == 0 else \
                    {XT_AT + n: j for j, n in enumerate(QK1_SLOTS)}
                return [(jobs[v],)] if v in jobs else []
            if name == "v":
                j = v - XT_AT - 1
                if ph == 0:
                    return [(j, 2)] if 0 <= j < 16 else []
                return [divmod(V1_SLOTS.index(j + 1), 2)] if j + 1 in V1_SLOTS else []
            if name in ("qk_out", "v_out", "qk_last", "v_last"):
                own = name.endswith("last")
                done = [j[0] for j in steps(name.split("_")[0], ph, v if own else v - 1)
                        if j[-1] or name[0] == "q"]
                return [(j,) for j in done if own == (ph == 0 and j == 15)]
            if name == "proj":
                q = v - SCORES
                if ph == 0:
                    return [(q // 2, (2 * (q % 2), 2 * (q % 2) + 1))] if 0 <= q < QUADS else []
                return {8: [(0, (0, 1))], 9: [(0, (2, 3))], 16: [(1, (0, 1))],
                        17: [(1, (2, 3))]}.get(q, [])
            if name == "residual":
                return [()] if v - SCORES == (QUADS - 1 if ph == 0 else QUADS + 1) else []
            if name == "bias":
                v -= SCORES + (QUADS if ph == 0 else QUADS + 1)
                return [(v,)] if 0 <= v < 2 else []
            if name == "stats":
                return [()] if v == 0 else []
            if name == "aggr":
                return [()] if v == 1 else []
            if name == "norm":
                return [()] if v == 2 else []
            if name in ("xt0", "xt1"):
                return [()] if v == XT_AT + int(name[2]) else []
            if name == "ctx":
                return [(v,)] if ph == 1 and 0 <= v < 4 else []
            raise ValueError(name)

        def run(order, does, ph, g, before, slots=PERIOD):
            for n in range(slots):
                for name, what, lags in order[before[0] if before and n < TURN else min(ph, 1)]:
                    for p, gg, v in ([(*before, n + PERIOD)] if before else []) + [(ph, g, n)]:
                        if p < 2 or name in ("stats", "aggr", "norm", "xt0", "xt1"):
                            for args in steps(what, p, v, lags[min(p, 1)]):
                                does[name](p, gg, *args)
                if name_extra := does.get("slot"):
                    name_extra(ph, g, n)

        def attentions(eng, order, does):
            run(order, does, 0, 0, None)
            with eng.Fori(1, GROUPS) as g:
                run(order, does, 0, g, (0, g - 1))
            run(order, does, 1, 0, (0, GROUPS - 1))
            with eng.Fori(1, GROUPS) as g:
                run(order, does, 1, g, (1, g - 1))
            run(order, does, 2, 0, (1, GROUPS - 1), DRAIN)

        DRAIN = 16
        TURN = 8
        LEAD = 4

        def v2(lo, job):
            return V2[:, job, lo, :, :].rearrange("p t (a h c) -> p (t a) h c", a=4, h=4)[:, :, 0:4:3, :]

        def v2_raw():
            return A1[:, :].rearrange("p (a h c) -> p a h c", h=2, c=DH2)

        def w_order(i):
            return [j for n in range(PERIOD) for j in weight_slots(n)].index(i) + 1

        def w_piece(j):
            return [i for n in range(PERIOD) for i in weight_slots(n)][j]

        def weight_slots(n):
            return {2: (0, 1, 2), 3: (3,), 4: (4,), 5: (5, 6), 6: (7, 8), 7: (9, 10),
                    8: (11, 12), 9: (13,), 10: (14,), 11: (15,), 12: (16,), 13: (17,), 14: (18,),
                    15: (19,)}.get(n, ())

        QK1_SLOTS, V1_SLOTS = (1, 2, 7, 8), (3, 5, 10, 13)

        PE_ORDER = (
            (("scores", "quad", (0, 0)), ("xt1", "xt1", (0, 0)), ("proj", "proj", (4, 5)),
             ("pv", "quad", (2, 4)), ("transpose", "quad", (1, 3)), ("v", "v", (0, 0)),
             ("qk", "qk", (0, 0)), ("xt0", "xt0", (0, 0))),
            (("transpose", "quad", (1, 3)), ("scores", "quad", (0, 0)), ("xt1", "xt1", (0, 0)),
             ("proj", "proj", (4, 5)), ("v", "v", (0, 0)), ("xt0", "xt0", (0, 0)),
             ("pv", "quad", (2, 4)), ("qk", "qk", (0, 0))))
        ACT_ORDER = (
            (("probs", "quad", (2, 3)), ("xt1", "xt1", (0, 0)), ("v", "v_out", (0, 0)),
             ("qk", "qk_out", (0, 0)), ("exp", "quad", (0, 1)), ("out", "quad", (2, 4)),
             ("v", "v_last", (0, 0)), ("qk", "qk_last", (0, 0)), ("xt0", "xt0", (0, 0))),
            (("probs", "quad", (2, 3)), ("xt1", "xt1", (0, 0)), ("v", "v_out", (0, 0)),
             ("qk", "qk_out", (0, 0)), ("exp", "quad", (0, 1)), ("xt0", "xt0", (0, 0)),
             ("out", "quad", (2, 4))))
        DVE_ORDER = (
            (("inverse", "quad", (1, 2)), ("out", "quad", (3, 5)), ("probs", "quad", (2, 3)),
             ("xt1", "xt1", (0, 0)), ("max", "quad", (0, 1)), ("residual", "residual", (4, 5)),
             ("v", "v_out", (0, 0)), ("qk", "qk_out", (0, 0)), ("stats", "stats", (0, 0)),
             ("aggr", "aggr", (0, 0)), ("norm", "norm", (0, 0)), ("v", "v_last", (0, 0)),
             ("qk", "qk_last", (0, 0)), ("xt0", "xt0", (0, 0))),
            (("max", "quad", (0, 1)), ("inverse", "quad", (1, 2)), ("out", "quad", (3, 5)),
             ("probs", "quad", (2, 3)), ("xt1", "xt1", (0, 0)), ("residual", "residual", (4, 5)),
             ("v", "v_out", (0, 0)), ("qk", "qk_out", (0, 0)), ("stats", "stats", (0, 0)),
             ("aggr", "aggr", (0, 0)), ("norm", "norm", (0, 0)), ("xt0", "xt0", (0, 0))))
        POOL_ORDER = (
            (("normalise", "quad", (1, 2)), ("bias", "bias", (4, 5)), ("ctx", "ctx", (0, 0)),
             ("aggr", "aggr", (0, 0))),
            (("normalise", "quad", (1, 2)), ("bias", "bias", (4, 5)), ("aggr", "aggr", (0, 0)),
             ("ctx", "ctx", (0, 0))))

        block = ctx.enter_context(nc.Block())

        @block.sync
        def _(sp):
            def tokens(g):
                sp.dma_start(xs[:, TILES * g:TILES * (g + 1), :], x[g]).then_inc(x_in[g > 0], 16)

            tokens(0)
            for i in range(4):
                sp.dma_start(wst[:, i, :], pieces[w_piece(i)]).then_inc(w_in[i], 16)
            sp.dma_start(b2raw, rows[0:1, 2 * D + 2 * EXPERTS:2 * D + 2 * EXPERTS + EXPERTS * D].to_broadcast(
                [P, EXPERTS * D])).then_inc(b2_in, 16)
            for j in range(4, N1 + N2):
                sp.wait_ge(w_split, j - 3)
                sp.dma_start(wst[:, j % 4, :], pieces[w_piece(j)]).then_inc(w_in[j % 4], 16)
                if 6 <= j < 5 + GROUPS:
                    tokens(j - 5)

            def context(g):
                sp.dma_start(craw[:, :].rearrange("p (k t) -> p k t", k=KD),
                             ctxT[g]).then_inc(c_in, 16)

            def experts(g):
                for j in range(4):
                    if isinstance(g, int):
                        sp.wait_ge(w_split, N1 + N2 - 3 + j)
                    else:
                        sp.wait_ge(e_split, g * 4 + j - 3)
                    sp.dma_start(wst[:, j, :], pieces[N1 + N2 + g * 4 + j]).then_inc(w_in[j], 16)

            context(0)
            with sp.Fori(1, GROUPS) as g:
                sp.wait_ge(c_lo, nth(CTX, 1, g, -1))
                context(g)
            experts(0)
            with sp.Fori(1, MCH // 4) as g:
                experts(g)
            with sp.Fori(0, GROUPS) as g:
                sp.wait_ge(fin, g + 1)
                sp.dma_start(out[g], yo).then_inc(out_dma, 16)
            sp.wait_ge(out_dma, GROUPS * 16)

        @block.tensor
        def _(pe):
            def three(acc, lhs, rhs, first=True, last=True, shared=False):
                for i, (a, b) in enumerate(((0, 0), (0, 1), (1, 0))):
                    mm = pe.matmul(acc, lhs[a], rhs[b], start=first and i == 0,
                                   stop=last and i == 2, skip_group_check=shared)
                return mm

            def project_qk(ph, g, job):
                c, is_k = job // 2, (job + (ph == 0)) % 2
                pe.wait_ge(qk_lo, nth(QK_F1, ph, g, job - 1))
                if job == 0:
                    pe.wait_ge(xt_lo, nth(GRP, ph, g, 0))
                if ph == 1 and job == 1:
                    pe.wait_ge(c_lo, nth(CTX, 1, g, 0))
                i = 4 * (c // 2) + is_k if ph == 0 else N1 + is_k
                col = (c % 2) * P
                pe.wait_ge(w_split, w_order(i))
                src = CT if ph == 1 and is_k else XT
                biased = ph == 1 and is_k
                if biased:
                    if isinstance(g, int) and job == 1:
                        pe.wait_ge(ready_v, 2)
                    pe.matmul(A0[:, :], bkrow[:, c * P:(c + 1) * P], ones[:, :], start=True, stop=False)
                for k in range(KD):
                    mm = three(A0[:, :], [piece(i, s, k, col, col + P) for s in (0, 1)],
                               [src[:, s, k, :] for s in (0, 1)], k == 0 and not biased, k == KD - 1)
                mm.then_inc(qk_ps, 1)

            def project_v(ph, g, job, part):
                if part != 1:
                    pe.wait_ge(v_lo, nth(VJ_F1, ph, g, job - 1))
                if ph == 0:
                    if job == 0:
                        pe.wait_ge(xt_lo, nth(GRP, ph, g, 0))
                    i, src, width, col = 4 * (job // 4) + 2, XT, 256, 0
                    tiles = [(job % 4, 0)]
                else:
                    if job == 0:
                        pe.wait_ge(c_lo, nth(CTX, 1, g, 0))
                    i, src, width, col = N1 + 2, CT, P, job * P
                    tiles = [(t, t * P) for t in (2 * part, 2 * part + 1)]
                pe.wait_ge(w_split, w_order(i))
                for t, to in tiles:
                    for k in range(KD):
                        mm = three(A1[:, to:to + width],
                                   [src[:, s, k, t * P:(t + 1) * P] for s in (0, 1)],
                                   [piece(i, s, k, col, col + width) for s in (0, 1)],
                                   k == 0, k == KD - 1)
                if part:
                    mm.then_inc(v_ps, 1)

            def scores(ph, g, n):
                c = n // 2
                if ph == 0:
                    r, rows = c % 2, slice(0, P)
                    if n % 2 == 0:
                        pe.wait_ge(qk_lo, nth(QK_F1, ph, g, 2 * c + 1))
                else:
                    r, rows = c // 4, slice(32 * (c % 4), 32 * (c % 4) + 32)
                    if n % 8 == 0:
                        pe.wait_ge(qk_lo, nth(QK_F1, ph, g, 2 * r + 1))
                pe.wait_ge(exped, nth(SLOT_F2, ph, g, n - 2))
                if ph == 1:
                    pe.sem_inc(pe_gate, 1)
                for j in range(2):
                    b = 2 * (n % 2) + j
                    mm = three(S[n % 2][:, 256 * j:256 * (j + 1)],
                               [Q[rows, r, s, b * P:(b + 1) * P] for s in (0, 1)],
                               [K[rows, r, s, b, :, :].rearrange("p h c -> p (h c)") for s in (0, 1)])
                mm.then_inc(scores_ps, 1)

            def transpose_probs(ph, g, n):
                pe.wait_ge(normed, nth(SLOT, ph, g, n))
                pe.wait_ge(pt_lo, nth(SLOT_F1, ph, g, n - 1))
                for u in range(4):
                    mm = pe.transpose(T[:, u * P:(u + 1) * P], probs[:, n % 4, u * P:(u + 1) * P],
                                      ident[:, :])
                mm.then_inc(pt_ps, 1)

            def probs_v(ph, g, n):
                c = n // 2
                pe.wait_ge(pt_lo, nth(SLOT_F1, ph, g, n))
                if ph == 0 or n % 2 == 0:
                    pe.wait_ge(o_lo, nth(OUT_F1, ph, g, (n if ph == 0 else n // 2) - 1))
                if ph == 0:
                    cp = c // 2
                    if n % 4 < 2:
                        pe.wait_ge(v_lo, nth(VJ_F1, ph, g, 4 * cp + 2 * (n % 2) + 1))
                    for u in range(4):
                        b, h = 2 * (n % 2) + u // 2, u % 2
                        col = (c % 2) * P + h * DH1
                        mm = three(O[0:DH1, u * P:(u + 1) * P],
                                   [V[:, cp % 2, s, b, col:col + DH1] for s in (0, 1)],
                                   [PT[:, n % 2, s, u * P:(u + 1) * P] for s in (0, 1)])
                else:
                    if n % 8 == 0:
                        pe.wait_ge(v_lo, nth(VJ_F1, ph, g, n // 8))
                    for u in range(4):
                        b, h = 2 * (n % 2) + u // 2, u % 2
                        col = (2 * (c % 4) + h) * 32
                        mm = three(O[0:32, b * P:(b + 1) * P],
                                   [V2[:, c // 4, s, b, col:col + 32] for s in (0, 1)],
                                   [PT[:, n % 2, s, u * P:(u + 1) * P] for s in (0, 1)],
                                   h == 0, h == 1)
                mm.then_inc(pv_ps, 1)

            def project_out(ph, g, c, tiles):
                chunks = CHUNKS1 if ph == 0 else 2
                if ph == 0:
                    pe.wait_ge(o_lo, nth(OUT_F1, ph, g, 2 * c + tiles[0] // 2))
                    i, k = 4 * (c // 2) + 3, c % 2
                else:
                    pe.wait_ge(o_lo, nth(OUT_F1, ph, g, 4 * c + 3))
                    i, k = N1 + 3, c
                if c == 0:
                    pe.wait_ge(y_read, nth(GRP_F1, ph, g, -1))
                pe.wait_ge(w_split, w_order(i))
                for t in tiles:
                    mm = three(Y[t // 2][:, (t % 2) * D:(t % 2 + 1) * D],
                               [AT[:, c % 2, s, t * P:(t + 1) * P] for s in (0, 1)],
                               [piece(i, s, k, 0, D) for s in (0, 1)],
                               c == 0 and t % 2 == 0, c == chunks - 1, True)
                if tiles[-1] == TILES - 1:
                    mm.then_inc(oproj, 1)

            def transpose_tokens(ph, g, banks, free, halves=range(KD)):
                pe.wait_ge(ln_x, nth(GRP, ph, g, 0))
                for k in halves:
                    if free[k]:
                        pe.wait_ge(*free[k])
                    for t in range(TILES):
                        mm = pe.transpose(banks[k][:, t * P:(t + 1) * P], xn[:, t, k * P:(k + 1) * P],
                                          ident[:, :])
                    mm.then_inc(xt_ps, 1)

            def transpose_group(ph, g, k):
                free = (None, None) if ph == 0 and isinstance(g, int) and g == 0 else \
                    ((v_lo, nth(VJ_F1, ph, g, -1)), (qk_lo, nth(QK_F1, ph, g, -1)))
                transpose_tokens(ph, g, (A1, A0), free, (k,))

            pe.wait_ge(ready, 2)
            attentions(pe, PE_ORDER, {
                "scores": scores, "transpose": transpose_probs, "pv": probs_v, "proj": project_out,
                "qk": project_qk, "v": project_v,
                "xt0": lambda ph, g: transpose_group(ph, g, 0),
                "xt1": lambda ph, g: transpose_group(ph, g, 1)})

            def up(g, m):
                pe.wait_ge(act_done, nth(MSTEP_F4, 2, g, m - 4))
                if m == 0:
                    pe.wait_ge(xt_lo, nth(GRP, 2, g, 0))
                pe.wait_ge(e_split, m + 1)
                for k in range(KD):
                    mm = three(H[m % 4][:, :], [arena[:, m * 2 * PIECE + s * PIECE + k * P:
                                                      m * 2 * PIECE + s * PIECE + (k + 1) * P]
                                                for s in (0, 1)],
                               [XT[:, s, k, :] for s in (0, 1)], k == 0, k == KD - 1)
                mm.then_inc(f1_ps, 1)

            def down(g, m):
                pe.wait_ge(h_lo, nth(MSTEP_F4, 2, g, m))
                if m == 0:
                    pe.wait_ge(y_read, nth(GRP_F1, 2, g, -1))
                for t in range(TILES):
                    mm = three(Y[t // 2][:, (t % 2) * D:(t % 2 + 1) * D],
                               [PT[:, m % 2, s, t * P:(t + 1) * P] for s in (0, 1)],
                               [piece(m, s, 1, 0, D) for s in (0, 1)],
                               m == 0 and t % 2 == 0, m == MCH - 1, True)
                mm.then_inc(f2_ps, 1)

            def logits(g):
                pe.wait_ge(xt_lo, nth(GRP, 2, g, 0))
                for t in range(TILES):
                    for i, (k, s) in enumerate(((0, 0), (0, 1), (1, 0), (1, 1))):
                        mm = pe.matmul(T[:, t * 2 * EXPERTS:(t + 1) * 2 * EXPERTS],
                                       XT[:, s, k, t * P:(t + 1) * P],
                                       gate[:, k, :, :].rearrange("p s e -> p (s e)"),
                                       start=i == 0, stop=i == 3)
                mm.then_inc(lg_ps, 1)

            def experts(g):
                last = isinstance(g, int) and g == GROUPS - 1
                for m in range(MCH + 2):
                    if m == MCH - 1 and not last:
                        transpose_tokens(2, g + 1, (T, O), ((lg_v, g * LGV + 1), None))
                    if m < MCH:
                        up(g, m)
                    if m == 1:
                        logits(g)
                    if m >= 2:
                        down(g, m - 2)

            with pe.Fori(0, GROUPS - 1) as g:
                experts(g)
            experts(GROUPS - 1)

        @block.scalar
        def _(act):
            act.dma_start(bias[:, :], biases).then_inc(b_in, 16)
            act.dma_start(rowc[:, :], rows[0:1, 0:2 * D + 2 * EXPERTS].to_broadcast(
                [P, 2 * D + 2 * EXPERTS])).then_inc(b_in, 16)
            at = 2 * D + 2 * EXPERTS + EXPERTS * D
            act.dma_start(bkraw[:, :], rows[0:1, at:at + D].to_broadcast([2, D])).then_inc(b_in, 16)
            act.dma_start(msk[:, :], mask).then_inc(b_in, 16)
            act.dma_start(gst[:, :], gateT).then_inc(b_in, 16)

            def tokens_hi(ph, g, banks, halves=range(KD)):
                for k in halves:
                    act.wait_ge(xt_ps, nth(XTE, ph, g, k))
                    act.activation(XT[:, 0, k, :], banks[k][:, :], ACT.Copy).then_inc(xt_hi, 1)

            def weight_hi(i):
                j = w_order(i) - 1
                act.wait_ge(w_in[j % 4], 16 * (j // 4 + 1))
                scale = (DH1 ** -0.5 if i < N1 and i % 4 == 0 else DH2 ** -0.5 if i == N1 else 1.0)
                act.activation(arena[:, i * 2 * PIECE:i * 2 * PIECE + PIECE], wst[:, j % 4, :], ACT.Copy,
                               scale=scale).then_inc(w_hi, 1)

            def qk_evac(ph, g, job):
                c, is_k = job // 2, (job + (ph == 0)) % 2
                if ph == 0 and isinstance(g, int) and g == 0 and job == 0:
                    act.wait_ge(ready_v, 2)
                    act.wait_ge(ready, 3)
                act.wait_ge(qk_ps, nth(QK, ph, g, job))
                if not is_k:
                    col = (BQ1 if ph == 0 else BQ2) + c
                    last = act.activation(Q[:, c % 2, 0, :], A0[:, :], ACT.Identity,
                                          bias=bias[:, col:col + 1])
                elif ph == 0:
                    for h in range(2):
                        rows_ = slice(h * DH1, (h + 1) * DH1)
                        last = act.activation(K[rows_, c % 2, 0, :, h, :],
                                              A0[rows_, :].rearrange("p (b c) -> p b c", b=TILES),
                                              ACT.Identity, bias=bias[rows_, BK1 + c:BK1 + c + 1])
                else:
                    for h in range(2):
                        last = act.activation(K[:, c % 2, 0, :, h, :],
                                              A0[:, :].rearrange("p (b c) -> p b c", b=TILES),
                                              ACT.Copy, scale=half[:, h:h + 1])
                last.then_inc(qk_hi, 1)

            def v_evac(ph, g, job):
                act.wait_ge(v_ps, nth(VJ, ph, g, job))
                if ph == 0:
                    cp, t = job // 4, job % 4
                    if t == 0 and (cp > 1 or not (isinstance(g, int) and g == 0)):
                        act.wait_ge(pv_ps, nth(SLOT_F2, ph, g, 4 * (cp - 1) - 1))
                    act.activation(V[:, cp % 2, 0, t, :], A1[:, 0:256], ACT.Copy).then_inc(v_hi, 1)
                else:
                    if isinstance(g, int):
                        act.wait_ge(v_zero, 2 * (job + 1))
                    else:
                        act.wait_ge(pv_ps, nth(SLOT_F2, ph, g, 8 * (job - 1) - 1))
                    act.activation(v2(0, job), v2_raw(), ACT.Copy).then_inc(v_hi, 1)

            def xt_evac(ph, g, k):
                tokens_hi(ph, g, (A1, A0), (k,))

            def exp_probs(ph, g, n):
                act.wait_ge(maxed, nth(SLOT, ph, g, n))
                if (ph, n) == (0, 0) and isinstance(g, int):
                    act.wait_ge(b2_sum, 3)
                act.wait_ge(pt_ps, nth(SLOT_F4, ph, g, n - 4))
                for u in range(4):
                    last = act.activation(probs[:, n % 4, u * P:(u + 1) * P],
                                          S[n % 2][:, u * P:(u + 1) * P], ACT.Exp,
                                          bias=nm[:, n % 4, u:u + 1], accum_out=rsum[:, n % 4, u:u + 1])
                last.then_inc(exped, 1)

            def probs_hi(ph, g, n):
                act.wait_ge(pt_ps, nth(SLOT_F4, ph, g, n))
                act.wait_ge(pv_ps, nth(SLOT_F2, ph, g, n - 2))
                act.activation(PT[:, n % 2, 0, :], T[:, :], ACT.Copy).then_inc(pt_hi, 1)

            def out_hi(ph, g, n):
                c = n // 2
                if ph == 1 and n % 2 == 0:
                    return
                act.wait_ge(pv_ps, nth(SLOT_F2, ph, g, n))
                if ph == 0:
                    if n % 2 == 0:
                        act.wait_ge(oproj, nth(OPROJ, ph, g, c - 2))
                    for h in range(2):
                        last = act.activation(
                            AT[h * DH1:(h + 1) * DH1, c % 2, 0, (n % 2) * 256:(n % 2 + 1) * 256]
                            .rearrange("p (b c) -> p b c", b=2),
                            O[0:DH1, :].rearrange("p (b h c) -> p b h c", b=2, h=2)[:, :, h, :],
                            ACT.Identity, bias=bias[0:DH1, BV1 + 2 * c + h:BV1 + 2 * c + h + 1])
                else:
                    if c % 4 == 0:
                        act.wait_ge(oproj, nth(OPROJ, ph, g, c // 4 - 2))
                    last = act.activation(AT[32 * (c % 4):32 * (c % 4) + 32, c // 4, 0, :], O[0:32, :],
                                          ACT.Identity, bias=bias[0:32, BV2 + c:BV2 + c + 1])
                last.then_inc(o_hi, 1)

            def expert_hi(m):
                at = m * 2 * PIECE
                act.wait_ge(w_in[m % 4], 16 * ((N1 + N2 + m) // 4 + 1))
                act.activation(arena[:, at:at + PIECE], wst[:, m % 4, :], ACT.Copy).then_inc(e_hi, 1)

            def weights(ph, g, n):
                if ph == 2 and DRAIN - LEAD <= n < DRAIN:
                    if n == DRAIN - LEAD:
                        act.wait_ge(pv_ps, nth(SLOT_F2, 1, GROUPS - 1, QUADS - 1))
                    expert_hi(n - DRAIN + LEAD)
                if ph == 0 and isinstance(g, int):
                    for i in weight_slots(n):
                        weight_hi(i)
                    if n == 15:
                        act.activation(gate[:, :, 0, :], gst[:, :].rearrange("p (k e) -> p k e", k=KD),
                                       ACT.Copy).then_inc(w_hi, 1)

            attentions(act, ACT_ORDER, {
                "exp": exp_probs, "probs": probs_hi, "out": out_hi, "qk": qk_evac, "v": v_evac,
                "xt0": lambda ph, g: xt_evac(ph, g, 0), "xt1": lambda ph, g: xt_evac(ph, g, 1),
                "slot": weights})

            def experts(g):
                last = isinstance(g, int) and g == GROUPS - 1
                for m in range(MCH):
                    act.wait_ge(f1_ps, nth(MSTEP, 2, g, m))
                    act.wait_ge(h_lo, nth(MSTEP_F4, 2, g, m - 4))
                    act.activation(probs[:, m % 4, :], H[m % 4][:, :], ACT.Gelu,
                                   bias=bias[:, B1 + m:B1 + m + 1]).then_inc(act_done, 1)
                    act.wait_ge(act_done, nth(MSTEP_F4, 2, g, m))
                    act.wait_ge(f2_ps, nth(MSTEP_F2, 2, g, m - 2))
                    act.activation(PT[:, m % 2, 0, :], probs[:, m % 4, :], ACT.Copy).then_inc(h_hi, 1)
                    if isinstance(g, int) and g == 0 and m + LEAD < MCH:
                        expert_hi(m + LEAD)
                    if m == 12:
                        act.wait_ge(lg_v, g * LGV + 8)
                        act.activation(lg[:, 4, :], lg[:, 3, :], ACT.Exp, scale=2.0).then_inc(lg_exp, 1)
                if not last:
                    tokens_hi(2, g + 1, (T, O))

            experts(0)
            with act.Fori(1, GROUPS - 1) as g:
                experts(g)
            experts(GROUPS - 1)


        @block.vector
        def _(dve):
            def sub_lo(out_, src, hi, sem_):
                dve.tensor_tensor(out_, src, hi.bitcast(F32), ALU.subtract).then_inc(sem_, 1)

            def ln_stats(ph, g, t):
                tile_ = (g * TILES + t)
                dve.bn_stats(st[:, t, :], xs[:, tile_, :] if isinstance(tile_, int) else
                             xs[:, bass.ds(tile_, 1), :].rearrange("p a d -> p (a d)")
                             ).then_inc(ln_stat, 1)

            def ln_finish(ph, g):
                dve.wait_ge(ln_stat, nth(LNST, ph, g, TILES - 1))
                dve.sem_inc(dve_gate, 1)
                for t in range(TILES):
                    last = dve.bn_aggr(mv[:, t, :], st[:, t, :])
                last.then_inc(ln_aggr, 1)
                dve.wait_ge(ln_aggr, nth(GRP, ph, g, 0))
                dve.tensor_scalar(ve[:, :], mv[:, :, 1], LN_EPS, None, ALU.add).then_inc(ln_var, 1)

            def ln_apply(ph, g):
                dve.wait_ge(ln_rstd, nth(GRP, ph, g, 0))
                if not (ph == 0 and isinstance(g, int) and g == 0):
                    dve.wait_ge(xt_ps, nth(XTE, ph, g, -1))
                for t in range(TILES):
                    tile_ = g * TILES + t
                    src = xs[:, tile_, :] if isinstance(tile_, int) else \
                        xs[:, bass.ds(tile_, 1), :].rearrange("p a d -> p (a d)")
                    last = dve.tensor_scalar(xn[:, t, :], src, mv[:, t, 0:1], rstd[:, t:t + 1],
                                             ALU.subtract, ALU.mult)
                last.then_inc(ln_x, 1)

            def tokens_lo(ph, g, banks, halves=range(KD)):
                for k in halves:
                    dve.wait_ge(xt_hi, nth(XTE, ph, g, k))
                    last = dve.tensor_tensor(XT[:, 1, k, :], banks[k][:, :], XT[:, 0, k, :].bitcast(F32),
                                             ALU.subtract)
                    if k == KD - 1:
                        last.then_inc(xt_lo, 1)

            def weight_lo(i):
                dve.wait_ge(w_hi, w_order(i))
                scale = (DH1 ** -0.5 if i < N1 and i % 4 == 0 else DH2 ** -0.5 if i == N1 else 1.0)
                at = i * 2 * PIECE
                dve.scalar_tensor_tensor(arena[:, at + PIECE:at + 2 * PIECE],
                                         wst[:, (w_order(i) - 1) % 4, :], scale,
                                         arena[:, at:at + PIECE].bitcast(F32), ALU.mult,
                                         ALU.subtract).then_inc(w_split, 1)

            def qk_low(ph, g, job):
                c, is_k = job // 2, (job + (ph == 0)) % 2
                dve.wait_ge(qk_hi, nth(QK, ph, g, job))
                if not is_k:
                    col = (BQ1 if ph == 0 else BQ2) + c
                    last = dve.scalar_tensor_tensor(Q[:, c % 2, 1, :], A0[:, :], bias[:, col:col + 1],
                                                    Q[:, c % 2, 0, :].bitcast(F32), ALU.add, ALU.subtract)
                elif ph == 0:
                    for h in range(2):
                        rows_ = slice(h * DH1, (h + 1) * DH1)
                        last = dve.scalar_tensor_tensor(
                            K[rows_, c % 2, 1, :, h, :],
                            A0[rows_, :].rearrange("p (b c) -> p b c", b=TILES),
                            bias[rows_, BK1 + c:BK1 + c + 1],
                            K[rows_, c % 2, 0, :, h, :].bitcast(F32), ALU.add, ALU.subtract)
                else:
                    for h in range(2):
                        last = dve.scalar_tensor_tensor(
                            K[:, c % 2, 1, :, h, :], A0[:, :].rearrange("p (b c) -> p b c", b=TILES),
                            half[:, h:h + 1], K[:, c % 2, 0, :, h, :].bitcast(F32),
                            ALU.mult, ALU.subtract)
                last.then_inc(qk_lo, 1)

            def v_low(ph, g, job):
                dve.wait_ge(v_hi, nth(VJ, ph, g, job))
                if ph == 0:
                    r, t = job // 4 % 2, job % 4
                    sub_lo(V[:, r, 1, t, :], A1[:, 0:256], V[:, r, 0, t, :], v_lo)
                else:
                    sub_lo(v2(1, job), v2_raw(), v2(0, job), v_lo)

            def constants():
                dve.wait_ge(b_in, 80)
                dve.wait_ge(ready, 2)
                for h in range(2):
                    dve.tensor_reduce(half[:, h:h + 1],
                                      ident[:, :].rearrange("p (a h c) -> p a h c", a=4, h=2)[:, :, h, :],
                                      axis=AX.XY, op=ALU.add).then_inc(half_built, 1)
                dve.tensor_scalar(bias[:, BQ1:BQ1 + 8], bias[:, BQ1:BQ1 + 8], DH1 ** -0.5, None, ALU.mult)
                dve.tensor_scalar(bias[:, BQ2:BQ2 + 2], bias[:, BQ2:BQ2 + 2], DH2 ** -0.5, None, ALU.mult)
                dve.tensor_scalar(dropped[:, :], msk[:, :], 0.0, None, ALU.is_equal)
                dve.memset(neg[:, :], MASKED)
                dve.wait_ge(half_built, 2)
                dve.memset(ones[:, :].bitcast(F32), 1.0)
                dve.tensor_tensor(bkhi[:, :], bkraw[:, :], ident[0:2, 2:3].to_broadcast([2, D]),
                                  ALU.subtract).then_inc(half_built, 1)
                dve.wait_ge(half_built, 3)
                dve.tensor_tensor(bklo[:, :], bkraw[:, :], bkhi[:, :].bitcast(F32),
                                  ALU.subtract).then_inc(half_built, 1)
                dve.wait_ge(half_built, 4)
                dve.tensor_scalar(bklo[:, :], bklo[:, :], ident[0:2, 1:2], None, ALU.mult).then_inc(half_built, 1)
                dve.wait_ge(half_built, 5)
                dve.scalar_tensor_tensor(bkrow[:, :], bkhi[:, :].bitcast(F32), ident[0:2, 0:1], bklo[:, :],
                                         ALU.mult, ALU.add).then_inc(ready_v, 1)

            dve.memset(mhalf[:, :], -0.5).then_inc(ready_v, 1)

            def row_max(ph, g, n):
                dve.wait_ge(scores_ps, nth(SLOT, ph, g, n))
                s3 = S[n % 2][:, :].rearrange("p (u c) -> p u c", u=4)
                if ph == 1:
                    dve.sem_inc(dve_gate, 1)
                    dve.copy_predicated(s3, dropped[:, :].unsqueeze(1).to_broadcast([P, 4, P]),
                                        neg[:, :].unsqueeze(2).to_broadcast([P, 4, P])
                                        ).then_inc(filled, 1)
                    dve.wait_ge(filled, g * QUADS + n + 1)
                dve.tensor_reduce(nm[:, n % 4, :], s3, axis=AX.X, op=ALU.max, negate=True
                                  ).then_inc(maxed, 1)

            def row_inverse(ph, g, n):
                dve.wait_ge(exped, nth(SLOT_F2, ph, g, n))
                dve.reciprocal(rinv[:, n % 4, :], rsum[:, n % 4, :]).then_inc(inverted, 1)

            def probs_low(ph, g, n):
                dve.wait_ge(pt_hi, nth(SLOT, ph, g, n))
                sub_lo(PT[:, n % 2, 1, :], T[:, :], PT[:, n % 2, 0, :], pt_lo)

            def out_low(ph, g, n):
                c = n // 2
                if ph == 1 and n % 2 == 0:
                    return
                dve.wait_ge(o_hi, nth(OUT, ph, g, n if ph == 0 else c))
                o4 = O[:, :].rearrange("p (b h c) -> p b h c", b=2, h=2)
                cols = slice((n % 2) * 256, (n % 2 + 1) * 256)
                if ph == 0:
                    for h in range(2):
                        rows_ = slice(h * DH1, (h + 1) * DH1)
                        last = dve.scalar_tensor_tensor(
                            AT[rows_, c % 2, 1, cols].rearrange("p (b c) -> p b c", b=2),
                            o4[0:DH1, :, h, :], bias[0:DH1, BV1 + 2 * c + h:BV1 + 2 * c + h + 1],
                            AT[rows_, c % 2, 0, cols].rearrange("p (b c) -> p b c", b=2).bitcast(F32),
                            ALU.add, ALU.subtract)
                else:
                    rows_ = slice(32 * (c % 4), 32 * (c % 4) + 32)
                    last = dve.scalar_tensor_tensor(
                        AT[rows_, c // 4, 1, :], O[0:32, :], bias[0:32, BV2 + c:BV2 + c + 1],
                        AT[rows_, c // 4, 0, :].bitcast(F32), ALU.add, ALU.subtract)
                last.then_inc(o_lo, 1)

            def add_residual(ph, g):
                dve.wait_ge(oproj, nth(OPROJ, ph, g, OPROJ.per[ph] - 1))
                for j in range(2):
                    at = g * TILES + 2 * j
                    dst = xs[:, bass.ds(at, 2), :] if not isinstance(at, int) else xs[:, at:at + 2, :]
                    last = dve.tensor_tensor(dst, Y[j][:, :].rearrange("p (t d) -> p t d", t=2), dst,
                                             ALU.add)
                last.then_inc(y_read, 1)

            def stats(ph, g):
                if ph == 0:
                    dve.wait_ge(x_in[not (isinstance(g, int) and g == 0)],
                                16 if isinstance(g, int) and g == 0 else (GROUPS - 1) * 16)
                else:
                    dve.wait_ge(x_ready, nth(GRP, ph - 1, g, 0))
                    dve.sem_inc(dve_gate, 1)
                for t in range(TILES):
                    ln_stats(ph, g, t)

            def xt_low(ph, g, k):
                tokens_lo(ph, g, (A1, A0), (k,))

            def expert_lo(m):
                at = m * 2 * PIECE
                dve.wait_ge(e_hi, m + 1)
                sub_lo(arena[:, at + PIECE:at + 2 * PIECE], wst[:, m % 4, :], arena[:, at:at + PIECE],
                       e_split)

            def weights(ph, g, n):
                if ph == 2 and DRAIN - LEAD <= n < DRAIN:
                    expert_lo(n - DRAIN + LEAD)
                if ph == 0 and isinstance(g, int):
                    late = weight_slots(n) if n < 8 else weight_slots(n - 1) if n > 8 else ()
                    for i in late + (weight_slots(n) if n == PERIOD - 1 else ()):
                        weight_lo(i)
                    if g == 0 and n == XT_AT:
                        constants()
                    if n == 15:
                        dve.wait_ge(w_hi, N1 + N2 + 1)
                        sub_lo(gate[:, :, 1, :], gst[:, :].rearrange("p (k e) -> p k e", k=KD),
                               gate[:, :, 0, :], w_split)

            attentions(dve, DVE_ORDER, {
                "max": row_max, "inverse": row_inverse, "probs": probs_low, "out": out_low,
                "qk": qk_low, "v": v_low, "residual": add_residual, "stats": stats,
                "aggr": ln_finish, "norm": ln_apply, "xt0": lambda ph, g: xt_low(ph, g, 0),
                "xt1": lambda ph, g: xt_low(ph, g, 1), "slot": weights})

            def gating(g, step):
                def after(n):
                    dve.wait_ge(lg_v, g * LGV + n)

                def l3(i):
                    return lg[:, i, :].rearrange("p (t e) -> p t e", t=TILES)

                def row(i):
                    return rowc[:, 2 * D + i * EXPERTS:2 * D + (i + 1) * EXPERTS].unsqueeze(1) \
                        .to_broadcast([P, TILES, EXPERTS])

                def col(i):
                    return gs[:, i, :].unsqueeze(2).to_broadcast([P, TILES, EXPERTS])

                if step == 0:
                    dve.wait_ge(lg_ps, g + 1)
                    t4 = T[:, 0:TILES * 2 * EXPERTS].rearrange("p (t s e) -> p t s e", t=TILES, s=2)
                    dve.tensor_tensor(l3(4), t4[:, :, 0, :], row(0), ALU.add).then_inc(lg_a, 1)
                    dve.wait_ge(lg_a, g + 1)
                    dve.tensor_tensor(l3(0), t4[:, :, 1, :], l3(4), ALU.add).then_inc(lg_v, 1)
                elif step == 1:
                    after(1)
                    dve.tensor_tensor(lg[:, 1, :], lg[:, 0, :], lg[:, 0, :], ALU.mult).then_inc(lg_v, 1)
                elif step == 2:
                    after(2)
                    dve.tensor_reduce(gs[:, 0, :], l3(1), axis=AX.X, op=ALU.add).then_inc(lg_v, 1)
                elif step == 3:
                    after(3)
                    dve.tensor_scalar(gs[:, 1, :], gs[:, 0, :], 1.0 / EXPERTS, F32_EPS, ALU.mult,
                                      ALU.add).then_inc(lg_v, 1)
                elif step == 4:
                    dve.wait_ge(lg_pow, g + 1)
                    dve.tensor_tensor(l3(1), l3(0), col(2), ALU.mult).then_inc(lg_v, 1)
                elif step == 5:
                    after(5)
                    dve.tensor_tensor(l3(2), l3(1), row(1), ALU.mult).then_inc(lg_v, 1)
                elif step == 6:
                    after(6)
                    dve.tensor_reduce(gs[:, 3, :], l3(2), axis=AX.X, op=ALU.max).then_inc(lg_v, 1)
                elif step == 7:
                    after(7)
                    dve.tensor_tensor(l3(3), l3(2), col(3), ALU.subtract).then_inc(lg_v, 1)
                elif step == 8:
                    dve.wait_ge(lg_exp, g + 1)
                    dve.tensor_reduce(gs[:, 4, :], l3(4), axis=AX.X, op=ALU.add).then_inc(lg_v, 1)
                elif step == 9:
                    after(9)
                    dve.reciprocal(gs[:, 5, :], gs[:, 4, :]).then_inc(lg_v, 1)
                elif step == 10:
                    after(10)
                    dve.tensor_scalar(gs[:, 6, :], gs[:, 5, :], 1e-6, None, ALU.add).then_inc(lg_v, 1)
                elif step == 11:
                    after(11)
                    dve.reciprocal(gs[:, 3, :], gs[:, 6, :]).then_inc(lg_v, 1)
                elif step == 12:
                    after(12)
                    dve.tensor_tensor(gs[:, 7, :], gs[:, 5, :], gs[:, 3, :], ALU.mult).then_inc(ng_done, 1)

            def finish(g):
                dve.wait_ge(f2_ps, nth(MSTEP_F2, 2, g, MCH - 1))
                if not (isinstance(g, int) and g == 0):
                    dve.wait_ge(out_dma, g * 16)
                for j in range(2):
                    last = dve.tensor_tensor(yo[:, 2 * j:2 * j + 2, :],
                                             Y[j][:, :].rearrange("p (t d) -> p t d", t=2),
                                             b2sum[:, :].unsqueeze(1).to_broadcast([P, 2, D]), ALU.add)
                last.then_inc(y_read, 1)
                dve.wait_ge(y_read, nth(GRP_F1, 2, g, 0))
                dve.wait_ge(ng_done, g + 1)
                for t in range(TILES):
                    at = g * TILES + t
                    src = xs[:, at, :] if isinstance(at, int) else \
                        xs[:, bass.ds(at, 1), :].rearrange("p a d -> p (a d)")
                    last = dve.scalar_tensor_tensor(yo[:, t, :], yo[:, t, :], gs[:, 7, t:t + 1], src,
                                                    ALU.mult, ALU.add)
                last.then_inc(fin, 1)

            def experts(g):
                last = isinstance(g, int) and g == GROUPS - 1
                for m in range(MCH):
                    dve.wait_ge(h_hi, nth(MSTEP, 2, g, m))
                    sub_lo(PT[:, m % 2, 1, :], probs[:, m % 4, :], PT[:, m % 2, 0, :], h_lo)
                    if isinstance(g, int) and g == 0 and m + LEAD < MCH:
                        expert_lo(m + LEAD)
                    if 4 <= m <= 11:
                        gating(g, m - 4)
                    if 14 <= m <= 18:
                        gating(g, m - 6)
                    if not last:
                        if 20 <= m < 24:
                            if m == 20:
                                dve.wait_ge(x_ready, nth(GRP, 1, g + 1, 0))
                                dve.sem_inc(dve_gate, 1)
                            ln_stats(2, g + 1, m - 20)
                        if m == 24:
                            ln_finish(2, g + 1)
                        if m == 28:
                            ln_apply(2, g + 1)
                if not last:
                    tokens_lo(2, g + 1, (T, O))
                finish(g)

            experts(0)
            with dve.Fori(1, GROUPS - 1) as g:
                experts(g)
            experts(GROUPS - 1)

        @block.gpsimd
        def _(pool):
            for s, c in ((pt_ps, 4), (exped, 2), (pv_ps, 2), (pt_lo, 1), (o_lo, 1), (oproj, 2),
                         (qk_lo, 1), (v_lo, 1), (y_read, 1), (act_done, 4), (h_lo, 4), (f2_ps, 2)):
                pool.sem_inc(s, c)
            pool.memset(ident[:, :], 0.0).then_inc(ready, 1)
            pool.wait_ge(ready, 1)
            pool.affine_select(out=ident[:, :], in_=ident[:, :], compare_op=ALU.not_equal, fill=1.0,
                               base=0, pattern=[[-1, P]], channel_multiplier=1).then_inc(ready, 1)
            pool.memset(K.rearrange("p r s b h c -> p (r s b h c)").bitcast(F32), 0.0).then_inc(ready, 1)

            def inv_sqrt(ph, g):
                if ph == 0 and isinstance(g, int) and g == 0:
                    pool.wait_ge(ready_v, 1)
                pool.wait_ge(ln_var, nth(GRP, ph, g, 0))
                pool.tensor_tensor(rstd[:, :], ve[:, :], mhalf[:, :], ALU.pow).then_inc(ln_rstd, 1)

            def normalise(ph, g, n):
                pool.wait_ge(inverted, nth(SLOT, ph, g, n))
                p3 = probs[:, n % 4, :].rearrange("p (u c) -> p u c", u=4)
                pool.tensor_tensor(p3, p3, rinv[:, n % 4, :].unsqueeze(2).to_broadcast([P, 4, P]),
                                   ALU.mult).then_inc(normed, 1)

            def out_bias(ph, g, part):
                if part == 0:
                    pool.wait_ge(y_read, nth(GRP_F1, ph, g, 0))
                    pool.sem_inc(pool_gate, 1)
                at = g * TILES + 2 * part
                dst = xs[:, at:at + 2, :] if isinstance(at, int) else xs[:, bass.ds(at, 2), :]
                add = pool.tensor_tensor(dst, dst, rowc[:, ph * D:(ph + 1) * D].unsqueeze(1)
                                         .to_broadcast([P, 2, D]), ALU.add)
                if part == 1:
                    add.then_inc(x_ready, 1)

            def split_context(ph, g, part):
                k = part % 2
                raw, hi, lo = craw[:, k * GT:(k + 1) * GT], CT[:, 0, k, :], CT[:, 1, k, :]
                if part == 0:
                    pool.wait_ge(c_in, nth(CTX, 1, g, 0) * 16)
                    if not isinstance(g, int):
                        pool.wait_ge(qk_ps, nth(QK, 1, g, -1))
                        pool.wait_ge(v_ps, nth(VJ, 1, g, -1))
                    pool.sem_inc(pool_gate, 1)
                if part < 2:
                    rounded = pool.tensor_copy(hi, raw)
                    if part == 1:
                        rounded.then_inc(c_hi, 1)
                    return
                if part == 2:
                    pool.wait_ge(c_hi, nth(CTX, 1, g, 0))
                rest = pool.tensor_tensor(lo, raw, hi.bitcast(F32), ALU.subtract)
                if part == 3:
                    rest.then_inc(c_lo, 1)

            def once(ph, g, n):
                if ph == 1 and isinstance(g, int) and n < 4:
                    if n == 0:
                        pool.wait_ge(oproj, nth(OPROJ, 0, GROUPS - 1, 1))
                    pool.memset(arena[:, n * 1024:(n + 1) * 1024].bitcast(F32), 0.0).then_inc(v_zero, 1)
                if (ph, n) == (0, 1) and isinstance(g, int):
                    pool.wait_ge(b2_in, 16)
                    for i, w in enumerate((EXPERTS * D // 2, EXPERTS * D // 4)):
                        pool.tensor_tensor(b2raw[:, 0:w], b2raw[:, 0:w], b2raw[:, w:2 * w],
                                           ALU.add).then_inc(b2_sum, 1)
                        pool.wait_ge(b2_sum, i + 1)
                    pool.tensor_tensor(b2sum[:, :], b2raw[:, 0:D], b2raw[:, D:2 * D],
                                       ALU.add).then_inc(b2_sum, 1)

            attentions(pool, POOL_ORDER, {
                "slot": once,
                "normalise": normalise, "bias": out_bias, "ctx": split_context, "aggr": inv_sqrt})

            def inv_rms(g):
                pool.wait_ge(lg_v, g * LGV + 4)
                pool.tensor_tensor(gs[:, 2, :], gs[:, 1, :], mhalf[:, :], ALU.pow).then_inc(lg_pow, 1)

            inv_rms(0)
            inv_sqrt(2, 1)
            with pool.Fori(1, GROUPS - 1) as g:
                inv_rms(g)
                inv_sqrt(2, g + 1)
            inv_rms(GROUPS - 1)


_OUT = (16, 128, 256)


def kernel(**inputs):
    import numpy as np
    import concourse.bacc as bacc
    from concourse.bass_utils import run_bass_kernel_spmd as run

    f = {k: np.asarray(v) for k, v in inputs.items()}

    def halves(w):
        n = w.shape[1] // 256
        return w.reshape(2, P, n, 256).transpose(2, 1, 0, 3).reshape(n, P, PIECE)

    wq, wk, wv = (halves(f["L0_attn_W_" + c].reshape(HEADS * DH1, D).T) for c in "QKV")
    wo = f["L0_attn_W_O"].transpose(0, 2, 1).reshape(4, 2, P, D).transpose(0, 2, 1, 3).reshape(4, P, PIECE)
    first = np.stack([wq, wk, wv, wo], axis=1).reshape(N1, P, PIECE)
    second = np.concatenate([halves(f["L0_xattn_W" + c].T) for c in "qkvo"])
    w1 = f["L0_ffn_w1"].transpose(1, 0, 2).reshape(KD, P, MCH, P).transpose(2, 1, 0, 3).reshape(MCH, P, 256)
    w2 = f["L0_ffn_w2"].reshape(MCH, P, D)
    pieces = np.concatenate([first, second, np.concatenate([w1, w2], axis=2)])

    bv1 = np.concatenate([f["L0_attn_b_V"].reshape(HEADS, DH1).T] * 2)
    biases = np.concatenate(
        [f["L0_attn_b_Q"].reshape(8, P).T, f["L0_attn_b_K"].reshape(8, P).T, bv1]
        + [f["L0_xattn_bq"].reshape(2, P).T]
        + [np.tile(f["L0_xattn_bv"].reshape(8, 32).T, (4, 1))] + [f["L0_ffn_b1"].reshape(MCH, P).T], axis=1)
    rows = np.concatenate([f["L0_attn_b_O"], f["L0_xattn_bo"], f["L0_ffn_gate_b"], f["L0_ffn_rms_w"],
                           f["L0_ffn_b2"].reshape(-1), f["L0_xattn_bk"]]).reshape(1, -1)
    gateT = f["L0_ffn_gate_w"].T.reshape(KD, P, EXPERTS).transpose(1, 0, 2).reshape(P, KD * EXPERTS)
    x = f["x"].reshape(GROUPS, TILES, P, D).transpose(0, 2, 1, 3)
    ctxT = f["ctx_1024"].reshape(GROUPS, GT, KD, P).transpose(0, 3, 2, 1)
    mask = f["mask_1x1xSxS2_bk0"].reshape(P, P)

    nc = bacc.Bacc("TRN2", target_bir_lowering=False, num_devices=1)
    arrays, args = {}, []
    for name, a in (("x", x), ("ctxT", ctxT), ("mask", mask), ("pieces", pieces), ("gateT", gateT),
                    ("biases", biases), ("rows", rows)):
        a = np.ascontiguousarray(a)
        arrays["in_" + name] = a
        args.append(nc.dram_tensor("in_" + name, a.shape, mybir.dt.from_np(a.dtype),
                                   kind="ExternalInput").ap())
    args.append(nc.dram_tensor("out_0", (GROUPS, P, TILES, D), F32, kind="ExternalOutput").ap())
    build(nc, *args)
    got = run(nc, [arrays], core_ids=[0]).results[0]["out_0"]
    return got.transpose(0, 2, 1, 3).reshape(_OUT)
```
